# Optimizing a Trainium2 kernel written in Bass

```python
import numpy as np
import jax
import jax.numpy as jnp

def _softmax(x, axis=-1):
    return jax.nn.softmax(x, axis=axis)

def _gelu(x):
    return jax.nn.gelu(x, approximate=True)

def _silu(x):
    return jax.nn.silu(x)

def _sigmoid(x):
    return jax.nn.sigmoid(x)

def _layernorm(x, axis=-1, eps=1e-05):
    m = jnp.mean(x, axis=axis, keepdims=True)
    v = jnp.var(x, axis=axis, keepdims=True)
    return (x - m) / jnp.sqrt(v + eps)

def _scatter_add(tgt, idx, src, axis=0):
    return tgt.at[idx].add(src)

def _segment_sum(src, seg, n):
    return jax.ops.segment_sum(src, seg, n)
kernel_name = 'mk_gnn_resnorm_d1_gnn_r8_b2497d'

def setup_inputs(seed: int=0):
    np.random.seed(seed)
    _w = jnp.asarray

    def _rec_inputs():
        import jax
        import jax.numpy as jnp
        _gk = jax.random.key(seed)
        x = -0.000202 + 1 * jax.random.normal(jax.random.fold_in(_gk, 1), (6250, 128), jnp.float32)
        src = jax.random.randint(jax.random.fold_in(_gk, 2), (100000,), 0, 6250, jnp.int32)
        dst = jnp.minimum((6250 * jax.random.uniform(jax.random.fold_in(_gk, 3), (100000,)) ** 2.0).astype(jnp.int32), 49999)
        _o = jnp.argsort(dst, stable=True)
        src = src[_o]
        dst = dst[_o]
        edge_attr_64 = 0.000189758 + 1.00013 * jax.random.normal(jax.random.fold_in(_gk, 11), (100000, 64), jnp.float32)
        return (x, src, dst, edge_attr_64)
    x, src, dst, edge_attr_64 = _rec_inputs()

    def _L0_gnn_setup():
        import jax, jax.numpy as jnp
        import numpy as np
        N_NODES = 6250
        N_EDGES = 100000
        F_NODE = 128
        F_EDGE = 64
        Z_DIM = 2 * F_NODE + F_EDGE
        BN_EPS = 1e-05

        def _params(key):
            ks = jax.random.split(key, 16)
            s = 1.0 / np.sqrt(Z_DIM)
            p = {}
            for li, k4 in zip((1, 2), (ks[:8], ks[8:])):
                p[f'Wf{li}'] = jax.random.uniform(k4[0], (Z_DIM, F_NODE), jnp.float32, -s, s)
                p[f'bf{li}'] = jax.random.uniform(k4[1], (F_NODE,), jnp.float32, -s, s)
                p[f'Ws{li}'] = jax.random.uniform(k4[2], (Z_DIM, F_NODE), jnp.float32, -s, s)
                p[f'bs{li}'] = jax.random.uniform(k4[3], (F_NODE,), jnp.float32, -s, s)
                p[f'gamma{li}'] = jnp.ones((F_NODE,), jnp.float32)
                p[f'beta{li}'] = jnp.zeros((F_NODE,), jnp.float32)
                p[f'rmean{li}'] = jax.random.normal(k4[4], (F_NODE,), jnp.float32) * 0.1
                p[f'rvar{li}'] = jax.random.uniform(k4[5], (F_NODE,), jnp.float32, 0.5, 1.5)
            return p

        def _cgconv(x, src, dst, edge_attr, Wf, bf, Ws, bs, gamma, beta, rmean, rvar):
            z = jnp.concatenate([x[dst], x[src], edge_attr], axis=-1)
            msg = jax.nn.sigmoid(z @ Wf + bf) * jax.nn.softplus(z @ Ws + bs)
            n = x.shape[0]
            summed = jax.ops.segment_sum(msg, dst, num_segments=n)
            cnt = jax.ops.segment_sum(jnp.ones((dst.shape[0],), x.dtype), dst, num_segments=n)
            out = summed / jnp.maximum(cnt, 1.0)[:, None]
            out = (out - rmean) * jax.lax.rsqrt(rvar + BN_EPS) * gamma + beta
            return out + x
        key = jax.random.key(seed)
        k1, k2, k3, kp = jax.random.split(key, 4)
        inp = {'x': jax.random.normal(k1, (N_NODES, F_NODE), jnp.float32), 'edge_index': jax.random.randint(k2, (2, N_EDGES), 0, N_NODES, jnp.int64), 'edge_attr': jax.random.normal(k3, (N_EDGES, F_EDGE), jnp.float32)}
        inp.update(_params(kp))
        return inp
    _L0_gnn_all = _L0_gnn_setup()
    _L0_gnn_in = {k: v for k, v in _L0_gnn_all.items() if k in ('Wf1', 'bf1', 'Ws1', 'bs1', 'gamma1', 'beta1', 'rmean1', 'rvar1', 'Wf2', 'bf2', 'Ws2', 'bs2', 'gamma2', 'beta2', 'rmean2', 'rvar2')}
    del _L0_gnn_all
    return {'x': x, 'src': src, 'dst': dst, 'edge_attr_64': edge_attr_64, 'L0_gnn_Wf1': _L0_gnn_in['Wf1'], 'L0_gnn_bf1': _L0_gnn_in['bf1'], 'L0_gnn_Ws1': _L0_gnn_in['Ws1'], 'L0_gnn_bs1': _L0_gnn_in['bs1'], 'L0_gnn_gamma1': _L0_gnn_in['gamma1'], 'L0_gnn_beta1': _L0_gnn_in['beta1'], 'L0_gnn_rmean1': _L0_gnn_in['rmean1'], 'L0_gnn_rvar1': _L0_gnn_in['rvar1'], 'L0_gnn_Wf2': _L0_gnn_in['Wf2'], 'L0_gnn_bf2': _L0_gnn_in['bf2'], 'L0_gnn_Ws2': _L0_gnn_in['Ws2'], 'L0_gnn_bs2': _L0_gnn_in['bs2'], 'L0_gnn_gamma2': _L0_gnn_in['gamma2'], 'L0_gnn_beta2': _L0_gnn_in['beta2'], 'L0_gnn_rmean2': _L0_gnn_in['rmean2'], 'L0_gnn_rvar2': _L0_gnn_in['rvar2']}

def reference(x, src, dst, edge_attr_64, L0_gnn_Wf1, L0_gnn_bf1, L0_gnn_Ws1, L0_gnn_bs1, L0_gnn_gamma1, L0_gnn_beta1, L0_gnn_rmean1, L0_gnn_rvar1, L0_gnn_Wf2, L0_gnn_bf2, L0_gnn_Ws2, L0_gnn_bs2, L0_gnn_gamma2, L0_gnn_beta2, L0_gnn_rmean2, L0_gnn_rvar2):
    import jax
    import jax.numpy as jnp

    def _L0_gnn_ref(x, edge_index, edge_attr, Wf1, bf1, Ws1, bs1, gamma1, beta1, rmean1, rvar1, Wf2, bf2, Ws2, bs2, gamma2, beta2, rmean2, rvar2):
        import jax, jax.numpy as jnp
        import numpy as np
        N_NODES = 6250
        N_EDGES = 100000
        F_NODE = 128
        F_EDGE = 64
        Z_DIM = 2 * F_NODE + F_EDGE
        BN_EPS = 1e-05

        def _params(key):
            ks = jax.random.split(key, 16)
            s = 1.0 / np.sqrt(Z_DIM)
            p = {}
            for li, k4 in zip((1, 2), (ks[:8], ks[8:])):
                p[f'Wf{li}'] = jax.random.uniform(k4[0], (Z_DIM, F_NODE), jnp.float32, -s, s)
                p[f'bf{li}'] = jax.random.uniform(k4[1], (F_NODE,), jnp.float32, -s, s)
                p[f'Ws{li}'] = jax.random.uniform(k4[2], (Z_DIM, F_NODE), jnp.float32, -s, s)
                p[f'bs{li}'] = jax.random.uniform(k4[3], (F_NODE,), jnp.float32, -s, s)
                p[f'gamma{li}'] = jnp.ones((F_NODE,), jnp.float32)
                p[f'beta{li}'] = jnp.zeros((F_NODE,), jnp.float32)
                p[f'rmean{li}'] = jax.random.normal(k4[4], (F_NODE,), jnp.float32) * 0.1
                p[f'rvar{li}'] = jax.random.uniform(k4[5], (F_NODE,), jnp.float32, 0.5, 1.5)
            return p

        def _cgconv(x, src, dst, edge_attr, Wf, bf, Ws, bs, gamma, beta, rmean, rvar):
            z = jnp.concatenate([x[dst], x[src], edge_attr], axis=-1)
            msg = jax.nn.sigmoid(z @ Wf + bf) * jax.nn.softplus(z @ Ws + bs)
            n = x.shape[0]
            summed = jax.ops.segment_sum(msg, dst, num_segments=n)
            cnt = jax.ops.segment_sum(jnp.ones((dst.shape[0],), x.dtype), dst, num_segments=n)
            out = summed / jnp.maximum(cnt, 1.0)[:, None]
            out = (out - rmean) * jax.lax.rsqrt(rvar + BN_EPS) * gamma + beta
            return out + x
        src, dst = (edge_index[0], edge_index[1])
        x = _cgconv(x, src, dst, edge_attr, Wf1, bf1, Ws1, bs1, gamma1, beta1, rmean1, rvar1)
        x = _cgconv(x, src, dst, edge_attr, Wf2, bf2, Ws2, bs2, gamma2, beta2, rmean2, rvar2)
        return x
    edge_index = jnp.stack([src, dst])
    x = _layernorm(x + _L0_gnn_ref(x, edge_index, edge_attr_64, L0_gnn_Wf1, L0_gnn_bf1, L0_gnn_Ws1, L0_gnn_bs1, L0_gnn_gamma1, L0_gnn_beta1, L0_gnn_rmean1, L0_gnn_rvar1, L0_gnn_Wf2, L0_gnn_bf2, L0_gnn_Ws2, L0_gnn_bs2, L0_gnn_gamma2, L0_gnn_beta2, L0_gnn_rmean2, L0_gnn_rvar2), axis=-1)
    return x

_drawn_inputs = setup_inputs


def setup_inputs(seed=0):
    import zlib

    import numpy as np

    out = dict(_drawn_inputs(seed))
    spreads = {'L0_gnn_gamma1': (1.0, 0.2),
     'L0_gnn_beta1': (0.0, 0.1),
     'L0_gnn_gamma2': (1.0, 0.2),
     'L0_gnn_beta2': (0.0, 0.1)}
    factors = {'edge_attr_64': 2.799,
     'L0_gnn_bf1': 8.0,
     'L0_gnn_bs1': 8.0,
     'L0_gnn_bf2': 8.0,
     'L0_gnn_bs2': 8.0}
    for name, (base, spread) in spreads.items():
        noise = np.random.default_rng([zlib.crc32(name.encode()), seed]).standard_normal(out[name].shape)
        drawn = base * np.exp(spread * noise) if base else spread * noise
        out[name] = jnp.asarray(drawn.astype(out[name].dtype))
    for name, factor in factors.items():
        out[name] = (out[name] * factor).astype(out[name].dtype)
    return out
```

```python
from contextlib import ExitStack

import numpy as np

import concourse.bass as bass
from concourse import mybir

ALU = mybir.AluOpType
ACT = mybir.ActivationFunctionType
AX = mybir.AxisListType
F32 = mybir.dt.float32
BF16 = mybir.dt.bfloat16
I32 = mybir.dt.int32
U32 = mybir.dt.uint32

P = 128
NODES = 6250
EDGES = 100000
F = 128
FE = 64
F2 = 2 * F
BN_EPS = 1e-5
LN_EPS = 1e-5

WINDOWS = -(-NODES // P)
WPAD = WINDOWS + WINDOWS % 2
NPAD = WPAD * P
TILES = 2
STEP = TILES * P
SLOTS = 4
EPAD = EDGES + 352
NO_WINDOW = NPAD + 1024
ECOLS = EPAD // P
SORTED_GROUPS = -(-((EDGES + WINDOWS * (STEP - 1)) // STEP) // SLOTS)
SORTED_STEPS = SORTED_GROUPS * SLOTS
SCOLS = -(-SORTED_STEPS // P)
BLOCKS = -(-EDGES // STEP)
GENERAL_GROUPS = -(-(BLOCKS * WINDOWS) // SLOTS)
GENERAL_STEPS = GENERAL_GROUPS * SLOTS
SORTED_AT = SLOTS
GENERAL_AT = SORTED_AT + SCOLS * P + SLOTS
TABLE = GENERAL_AT + GENERAL_STEPS


def plan_steps(nc, t, d):
    with nc.cleanup_on_exit(), ExitStack() as ctx:
        sb = lambda name, shape, dt: ctx.enter_context(nc.sbuf_tensor(name, shape, dt))
        sem = lambda name: nc.alloc_semaphore(name)
        dst_i = sb("dst_i", [P, 2, ECOLS], I32)
        dst_f = sb("dst_f", [P, 2, ECOLS], F32)
        below = sb("below", [P, ECOLS], F32)
        counts = sb("counts", [P, WINDOWS + 1], F32)
        ones = sb("ones", [P, P], F32)
        total = sb("total", [P, WINDOWS + 1], F32)
        in_window = sb("in_window", [P, WINDOWS], F32)
        steps_i = sb("steps_i", [P, WINDOWS], I32)
        steps_f = sb("steps_f", [P, WINDOWS], F32)
        step_end = sb("step_end", [P, WINDOWS], F32)
        shift = sb("shift", [P, WINDOWS], F32)
        step_no = sb("step_no", [P, SCOLS], F32)
        passed = sb("passed", [P, SCOLS, WINDOWS], F32)
        shifted = sb("shifted", [P, SCOLS, WINDOWS], F32)
        win_f = sb("win_f", [P, SCOLS], F32)
        off_f = sb("off_f", [P, SCOLS], F32)
        entry = sb("entry", [P, 2, SCOLS], I32)
        flag_f = sb("flag_f", [1, 4], F32)
        gen_off = sb("gen_off", [WINDOWS, BLOCKS], I32)
        gen_win = sb("gen_win", [WINDOWS, BLOCKS], I32)
        tail = sb("tail", [1, 2, SLOTS], I32)
        total_ps = ctx.enter_context(nc.psum_tensor("total_ps", [P, 512], F32))

        dst_in = sem("dst_in")
        iotas = sem("iotas")
        dve = sem("dve_done")
        summed = sem("summed")
        written = sem("written")
        general = t["off_dram"][GENERAL_AT:GENERAL_AT + WINDOWS * BLOCKS].rearrange("(w k) -> w k", k=BLOCKS)
        general_w = t["win_dram"][GENERAL_AT:GENERAL_AT + WINDOWS * BLOCKS].rearrange("(w k) -> w k", k=BLOCKS)
        rest = SLOTS * GENERAL_GROUPS - WINDOWS * BLOCKS
        sorted_off = t["off_dram"][SORTED_AT:SORTED_AT + SCOLS * P].rearrange("(p c) -> p c", c=SCOLS)
        sorted_win = t["win_dram"][SORTED_AT:SORTED_AT + SCOLS * P].rearrange("(p c) -> p c", c=SCOLS)

        block = ctx.enter_context(nc.Block())

        @block.sync
        def _(sp):
            sp.dma_start(dst_i[:, 0, :], d["dst"][0:EPAD].rearrange("(p c) -> p c", c=ECOLS)).then_inc(dst_in, 16)
            sp.dma_start(dst_i[:, 1, :], d["dst"][1:EPAD + 1].rearrange("(p c) -> p c", c=ECOLS)).then_inc(dst_in, 16)
            sp.wait_ge(iotas, 5)
            sp.dma_start(general, gen_off[:]).then_inc(written, 16)
            sp.dma_start(general_w, gen_win[:]).then_inc(written, 16)
            n = 2
            for table, k in ((t["off_dram"], 0), (t["win_dram"], 1)):
                for at, many in ((0, SLOTS), (GENERAL_AT - SLOTS, SLOTS), (TABLE - rest, rest)):
                    if many:
                        sp.dma_start(table[at:at + many].rearrange("(a c) -> a c", a=1),
                                     tail[:, k, 0:many]).then_inc(written, 16)
                        n += 1
            sp.wait_ge(dve, 1)
            sp.dma_start(sorted_off, entry[:, 0, :]).then_inc(written, 16)
            sp.dma_start(sorted_win, entry[:, 1, :]).then_inc(written, 16)
            sp.wait_ge(written, 16 * (n + 2))

        @block.gpsimd
        def _(pool):
            nc.gpsimd.iota(step_no[:], [[1, SCOLS]], base=0, channel_multiplier=SCOLS,
                           allow_small_or_imprecise_dtypes=True).then_inc(iotas, 1)
            nc.gpsimd.iota(gen_off[:], [[STEP, BLOCKS]], base=0, channel_multiplier=0).then_inc(iotas, 1)
            nc.gpsimd.iota(gen_win[:], [[0, BLOCKS]], base=0, channel_multiplier=1).then_inc(iotas, 1)
            nc.gpsimd.iota(tail[:, 0, :], [[0, SLOTS]], base=EDGES, channel_multiplier=0).then_inc(iotas, 1)
            nc.gpsimd.iota(tail[:, 1, :], [[0, SLOTS]], base=WINDOWS - 1, channel_multiplier=0).then_inc(iotas, 1)
            nc.gpsimd.iota(t["node_no"][:], [[1, WINDOWS * P]], base=0, channel_multiplier=0,
                           allow_small_or_imprecise_dtypes=True).then_inc(iotas, 1)

        @block.tensor
        def _(pe):
            pe.wait_ge(summed, 1)
            nc.tensor.matmul(total_ps[:, 0:WINDOWS + 1], ones[:], counts[:], start=True, stop=True).then_inc(summed, 1)

        @block.vector
        def _(v):
            own = sem("plan_chain")
            n = [0]

            def after(ins):
                n[0] += 1
                ins.then_inc(own, 1)
                v.wait_ge(own, n[0])

            nc.vector.memset(ones[:], 1.0)
            v.wait_ge(dst_in, 32)
            after(nc.vector.tensor_copy(dst_f[:], dst_i[:]))
            after(nc.vector.tensor_tensor(below[:], dst_f[:, 0, :], dst_f[:, 1, :], ALU.is_gt))
            after(nc.vector.tensor_reduce(counts[:, WINDOWS:WINDOWS + 1], below[:], AX.X, ALU.add))
            for w in range(WINDOWS):
                last = nc.vector.tensor_scalar(below[:], dst_f[:, 0, :], float(P * (w + 1)), None, ALU.is_lt,
                                               ALU.add, accum_out=counts[:, w:w + 1])
                after(last)
            v.sem_inc(summed, 1)
            v.wait_ge(summed, 2)
            after(nc.vector.tensor_copy(total[:], total_ps[:, 0:WINDOWS + 1]))
            nc.vector.tensor_copy(in_window[:, 0:1], total[:, 0:1])
            after(nc.vector.tensor_tensor(in_window[:, 1:], total[:, 1:WINDOWS], total[:, 0:WINDOWS - 1], ALU.subtract))
            after(nc.vector.tensor_scalar(steps_i[:], in_window[:], float(STEP - 1), None, ALU.add))
            after(nc.vector.tensor_scalar(steps_i[:], steps_i[:], STEP.bit_length() - 1, None, ALU.arith_shift_right))
            after(nc.vector.tensor_copy(steps_f[:], steps_i[:]))
            after(nc.vector.tensor_tensor_scan(step_end[:], steps_f[:], steps_f[:], 0.0, ALU.add, ALU.bypass))
            after(nc.vector.scalar_tensor_tensor(shift[:], steps_f[:], -float(STEP), in_window[:], ALU.mult, ALU.add))
            v.wait_ge(iotas, 6)
            for c in range(SCOLS):
                after(nc.vector.tensor_scalar(passed[:, c, :], step_end[:], step_no[:, c:c + 1], None, ALU.is_le))
                after(nc.vector.tensor_tensor(shifted[:, c, :], passed[:, c, :], shift[:], ALU.mult))
            after(nc.vector.tensor_reduce(win_f[:], passed[:], AX.X, ALU.add))
            after(nc.vector.tensor_reduce(off_f[:], shifted[:], AX.X, ALU.add))
            after(nc.vector.scalar_tensor_tensor(off_f[:], step_no[:], float(STEP), off_f[:], ALU.mult, ALU.add))
            after(nc.vector.tensor_scalar(entry[:, 0, :], off_f[:], float(EDGES), None, ALU.min))
            after(nc.vector.tensor_scalar(flag_f[:, 0:1], total[0:1, WINDOWS:WINDOWS + 1], 1.0, None, ALU.min))
            after(nc.vector.tensor_scalar(t["choice"][:, 0:1], flag_f[:, 0:1], float(GENERAL_GROUPS - SORTED_GROUPS),
                                          float(SORTED_GROUPS - 2), ALU.mult, ALU.add))
            after(nc.vector.tensor_scalar(t["choice"][:, 1:2], flag_f[:, 0:1], float(GENERAL_AT - SORTED_AT),
                                          None, ALU.mult))
            nc.vector.tensor_scalar(entry[:, 1, :], win_f[:], float(WINDOWS - 1), None, ALU.min).then_inc(dve, 1)
            v.wait_ge(dve, 1)


def layer_tables(nc, t, d, layer):
    with nc.cleanup_on_exit(), ExitStack() as ctx:
        sb = lambda name, shape, dt: ctx.enter_context(nc.sbuf_tensor(f"{name}{layer}", shape, dt))
        sem = lambda name: nc.alloc_semaphore(f"{name}{layer}")
        ps = lambda name, shape, dt: ctx.enter_context(nc.psum_tensor(f"{name}{layer}", shape, dt))
        second = layer == 2
        w_node = sb("w_node", [P, 2 * F2], F32)
        bias = sb("bias", [P, F2], F32)
        x_t = sb("x_t", [P, 2, P], F32)
        dst_part = sb("dst_part", [P, 2, F2], F32)
        rest = sb("rest", [P, 2, F2], F32)
        src_part = sb("src_part", [P, 2, F2], F32)
        scaled = sb("scaled", [P, 2, F], F32)
        x_new = sb("x_new", [P, 2, F], F32)
        dst_ps = ps("dst_ps", [P, 2, 512], F32)
        src_ps = ps("src_ps", [P, 2, 512], F32)
        turned = ps("turned", [P, 2, 512], F32)

        loaded = sem("weights_in")
        x_in = [sem(f"x_in{s}") for s in range(2)]
        x_ready = sem("x_ready")
        x_turned = sem("x_turned")
        x_scaled = sem("x_scaled")
        x_kept = sem("x_kept")
        prod_done = sem("prod_done")
        dst_done = sem("dst_done")
        part1 = sem("part1")
        rest1 = sem("rest1")
        part2 = sem("part2")
        part3 = sem("part3")
        src_done = sem("src_done")
        src_out = [sem(f"src_out{s}") for s in range(2)]
        W, parts, win3 = d[f"W{layer}"], t["dst_parts"], 3 * F2
        PAIRS = WPAD // 2

        block = ctx.enter_context(nc.Block())

        def windows(eng, step):
            for s in range(2):
                step(s, 0, s, True)
            with eng.Fori(1, PAIRS) as q:
                for s in range(2):
                    step(q * 2 + s, q, s, False)

        @block.sync
        def _(sp):
            sp.dma_start(w_node[:], W["node"]).then_inc(loaded, 16)
            sp.dma_start(bias[:], W["bias"].rearrange("(a f) -> a f", a=1).to_broadcast([P, F2])).then_inc(loaded, 16)

            def step(w, q, s, first):
                if not second:
                    if not first:
                        sp.wait_ge(prod_done, q * 2 + (s - 1))
                    sp.dma_start(x_t[:, s, :], d["xT"][:, bass.ds(w * P, P)]).then_inc(x_in[s], 16)
            if not second:
                windows(sp, step)

        @block.gpsimd
        def _(pool):
            def step(w, q, s, first):
                pool.wait_ge(src_done, q * 2 + (s + 1))
                pool.dma_start(t[f"src_dram{layer}"][bass.ds(w * P, P), :], src_part[:, s, :]).then_inc(src_out[s], 16)
            windows(pool, step)
            for s in range(2):
                pool.wait_ge(src_out[s], 16 * PAIRS)

        @block.tensor
        def _(pe):
            pe.wait_ge(loaded, 32)

            def step(w, q, s, first):
                if second:
                    pe.wait_ge(x_scaled, q * 2 + (s + 1))
                    nc.tensor.transpose(turned[:, s, 0:P], x_new[:, s, :], t["ident"][:]).then_inc(x_turned, 1)
                    pe.wait_ge(x_ready, q * 2 + (s + 1))
                else:
                    pe.wait_ge(x_in[s], q * 16 + 16)
                if not first:
                    pe.wait_ge(dst_done, q * 2 + (s - 1))
                    pe.wait_ge(src_done, q * 2 + (s - 1))
                nc.tensor.matmul(dst_ps[:, s, 0:F2], x_t[:, s, :], w_node[:, 0:F2], start=True, stop=True)
                nc.tensor.matmul(src_ps[:, s, 0:F2], x_t[:, s, :], w_node[:, F2:2 * F2], start=True, stop=True
                                 ).then_inc(prod_done, 1)
            windows(pe, step)

        @block.scalar
        def _(act):
            def step(w, q, s, first):
                if second:
                    act.wait_ge(x_turned, q * 2 + (s + 1))
                    if not first:
                        act.wait_ge(prod_done, q * 2 + (s - 1))
                    nc.scalar.copy(x_t[:, s, :], turned[:, s, 0:P]).then_inc(x_ready, 1)
                    nc.scalar.copy(t["x_nodes"][:, bass.ds(w * F, F)], x_new[:, s, :]).then_inc(x_kept, 1)
                act.wait_ge(prod_done, q * 2 + (s + 1))
                if not first:
                    act.wait_ge(src_out[s], q * 16)
                nc.scalar.copy(src_part[:, s, :], src_ps[:, s, 0:F2]).then_inc(src_done, 1)
                act.wait_ge(dst_done, q * 2 + (s + 1))
                nc.scalar.copy(parts[:, bass.ds(w * win3, F2)], dst_part[:, s, :]).then_inc(part1, 1)
                act.wait_ge(rest1, q * 2 + (s + 1))
                nc.scalar.copy(parts[:, bass.ds(w * win3 + F2, F2)], rest[:, s, :]).then_inc(part2, 1)
            windows(act, step)

        @block.vector
        def _(v):
            v.wait_ge(loaded, 32)

            def step(w, q, s, first):
                if second:
                    if not first:
                        v.wait_ge(x_turned, q * 2 + (s - 1))
                        v.wait_ge(x_kept, q * 2 + (s - 1))
                    nc.vector.scalar_tensor_tensor(
                        scaled[:, s, :], t["sums"][:, bass.ds(w * (F + 1), F)], t["per_count"][:, bass.ds(w, 1)],
                        t["bn_scale1"][:], ALU.mult, ALU.mult).then_inc(own, 1)
                    v.wait_ge(own, q * 2 + (s + 1))
                    nc.vector.tensor_tensor(x_new[:, s, :], t["x_nodes"][:, bass.ds(w * F, F)], scaled[:, s, :],
                                            ALU.add).then_inc(x_scaled, 1)
                v.wait_ge(prod_done, q * 2 + (s + 1))
                if not first:
                    v.wait_ge(part3, q * 2 + (s - 1))
                nc.vector.tensor_tensor(dst_part[:, s, :], dst_ps[:, s, 0:F2], bias[:], ALU.add).then_inc(dst_done, 1)
                v.wait_ge(part1, q * 2 + (s + 1))
                nc.vector.tensor_tensor(rest[:, s, :], dst_part[:, s, :], parts[:, bass.ds(w * win3, F2)],
                                        ALU.subtract).then_inc(rest1, 1)
                v.wait_ge(part2, q * 2 + (s + 1))
                nc.vector.tensor_tensor(parts[:, bass.ds(w * win3 + 2 * F2, F2)], rest[:, s, :],
                                        parts[:, bass.ds(w * win3 + F2, F2)], ALU.subtract).then_inc(part3, 1)
            own = sem("scaled")
            windows(v, step)


def edge_loop(nc, t, d, layer):
    with nc.cleanup_on_exit(), ExitStack() as ctx:
        sb = lambda name, shape, dt: ctx.enter_context(nc.sbuf_tensor(f"{name}{layer}", shape, dt))
        ps = lambda name, shape, dt: ctx.enter_context(nc.psum_tensor(f"{name}{layer}", shape, dt))
        sem = lambda name: nc.alloc_semaphore(f"{name}{layer}")
        each = lambda name: [nc.alloc_semaphore(f"{name}{layer}_{j}") for j in range(SLOTS)]

        w_edge = sb("w_edge", [FE, F2], F32)
        sp_off = sb("sp_off", [1, SLOTS], I32)
        wins = sb("wins", [1, 2 * SLOTS], I32)
        ends = sb("ends", [P, SLOTS, TILES, 2], I32)
        edge_t = sb("edge_t", [FE, SLOTS, STEP], F32)
        from_src = sb("from_src", [P, SLOTS, TILES, F2], F32)
        hot = sb("hot", [P, SLOTS, TILES, P], BF16)
        hot_t = sb("hot_t", [P, 2, TILES, P], BF16)
        hot_f = sb("hot_f", [P, 2, TILES, P], F32)
        pre = sb("pre", [P, 2, TILES, F2], F32)
        value = sb("value", [P, 2, TILES, F], F32)
        expo = sb("expo", [P, 2, TILES, F2], F32)
        logs = sb("logs", [P, 2, TILES, F2], F32)
        gate = sb("gate", [P, 2, TILES, F], F32)
        soft = sb("soft", [P, 2, TILES, F], F32)
        msg = sb("msg", [P, 2, TILES, F + 1], F32)
        turn_ps = ps("turn_ps", [P, 2, 1024], BF16)
        pre_ps = ps("pre_ps", [P, 2, TILES, F2], F32)
        sum_ps = ps("sum_ps", [P, 2, 512], F32)

        w_in = sem("w_edge_in")
        sp_tab = sem("sp_table_in")
        win_tab = sem("windows_in")
        pe_has = sem("pe_has_windows")
        dve_has = sem("dve_has_windows")
        ready = sem("ones_ready")
        passed = sem("waits_passed")
        ends_in, edge_in, src_in = each("ends_in"), each("edge_in"), each("src_in")
        s_hot, s_turn, s_hot_t, s_hot_f = each("hot_done"), each("turn_done"), each("hot_t_done"), each("hot_f_done")
        s_prod, s_pre, s_abs, s_expo = each("prod_done"), each("pre_done"), each("abs_done"), each("expo_done")
        s_logs, s_gate, s_soft, s_msg = each("logs_done"), each("gate_done"), each("soft_done"), each("msg_done")
        s_sum, s_added = each("sum_done"), each("added")

        max_w = WINDOWS - 1
        win3 = 3 * F2
        block = ctx.enter_context(nc.Block())

        def done(eng, sems, g, j, lag, each_inc=1):
            turns_back = (lag - j + SLOTS - 1) // SLOTS if lag > j else 0
            if isinstance(g, int):
                if g < turns_back:
                    return
                eng.wait_ge(sems[(j - lag) % SLOTS], (g - turns_back + 1) * each_inc)
            elif turns_back == 0:
                eng.wait_ge(sems[j - lag], g * each_inc + each_inc)
            else:
                eng.wait_ge(sems[(j - lag) % SLOTS], (g + (1 - turns_back)) * each_inc)

        def turns(eng, groups, one, drain):
            one(0)
            with eng.Fori(1, groups) as g:
                one(g)
            drain(groups)

        def n_groups(eng):
            return eng.value_load(t["choice"][:, 0:1], min_val=SORTED_GROUPS - 2, max_val=GENERAL_GROUPS - 2) + 2

        @block.sync
        def _(sp):
            sp.dma_start(w_edge[:], d[f"W{layer}"]["edge"]).then_inc(w_in, 16)
            groups = n_groups(sp)
            at = sp.value_load(t["choice"][:, 1:2], min_val=0, max_val=GENERAL_AT - SORTED_AT)
            row = lambda table, first, n: table[bass.ds(first, n)].rearrange("(a c) -> a c", a=1)
            sp.dma_start(sp_off[:], row(t["off_dram"], at + SORTED_AT, SLOTS)).then_inc(sp_tab, 16)
            sp.dma_start(wins[:], row(t["win_dram"], at, 2 * SLOTS)).then_inc(win_tab, 16)

            def one(g, last=False):
                sp.wait_ge(sp_tab, g * 16 + 16)
                sp.sem_inc(passed, 1)
                offs = [sp.value_load(sp_off[:, j:j + 1], min_val=0, max_val=EDGES) for j in range(SLOTS)]
                if not last:
                    sp.dma_start(sp_off[:], row(t["off_dram"], at + (g + 1) * SLOTS + SORTED_AT, SLOTS)
                                 ).then_inc(sp_tab, 16)
                for j in range(SLOTS):
                    done(sp, s_hot, g, j, SLOTS)
                    sp.sem_inc(passed, 1)
                    done(sp, src_in, g, j, SLOTS, 32)
                    sp.sem_inc(passed, 1)
                    sp.dma_start(ends[:, j, :, :], d["ends"][bass.ds(offs[j], STEP), :].rearrange(
                        "(p k) c -> p k c", k=TILES)).then_inc(ends_in[j], 16)
                    done(sp, s_prod, g, j, SLOTS)
                    sp.sem_inc(passed, 1)
                    sp.dma_start(edge_t[:, j, :], d["edge_t"][:, bass.ds(offs[j], STEP)]).then_inc(edge_in[j], 16)
                if not last:
                    sp.wait_ge(pe_has, g + 1)
                    sp.wait_ge(dve_has, g + 1)
                    sp.sem_inc(passed, 1)
                    sp.dma_start(wins[:], row(t["win_dram"], at + (g + 1) * SLOTS, 2 * SLOTS)).then_inc(win_tab, 16)

            one(0)
            with sp.Fori(1, groups - 1) as g:
                one(g)
            one(groups - 1, True)

        @block.gpsimd
        def _(pool):
            nc.gpsimd.memset(msg[:, :, :, F:F + 1], 1.0).then_inc(ready, 1)
            groups = n_groups(pool)

            def one(g):
                for j in range(SLOTS):
                    done(pool, ends_in, g, j, 0, 16)
                    done(pool, s_pre, g, j, SLOTS)
                    pool.sem_inc(passed, 1)
                    for k in range(TILES):
                        nc.gpsimd.indirect_dma_start(
                            from_src[:, j, k, :], None, t[f"src_dram{layer}"],
                            bass.IndirectOffsetOnAxis(ap=ends[:, j, k, 0:1], axis=0)).then_inc(src_in[j], 16)
            turns(pool, groups, one, lambda g: None)

        @block.tensor
        def _(pe):
            groups = n_groups(pe)
            pe.wait_ge(w_in, 16)

            def turn(g, j):
                done(pe, s_hot, g, j, 0)
                done(pe, s_hot_t, g, j, 2)
                for k in range(TILES):
                    ins = nc.tensor.transpose(turn_ps[:, j % 2, k * P:(k + 1) * P], hot[:, j, k, :], t["ident_b"][:])
                ins.then_inc(s_turn[j], 1)

            def product(g, j, win):
                done(pe, edge_in, g, j, 0, 16)
                done(pe, s_hot_t, g, j, 0)
                done(pe, s_pre, g, j, 2)
                for k in range(TILES):
                    nc.tensor.matmul(pre_ps[:, j % 2, k, :], edge_t[:, j, k:STEP:TILES], w_edge[:],
                                     start=True, stop=False)
                    for part in range(3):
                        ins = nc.tensor.matmul(pre_ps[:, j % 2, k, :], hot_t[:, j % 2, k, :],
                                               t["dst_parts"][:, bass.ds(win * win3 + part * F2, F2)],
                                               start=False, stop=part == 2)
                ins.then_inc(s_prod[j], 1)

            def window_sum(g, j):
                done(pe, s_hot_f, g, j, 0)
                done(pe, s_msg, g, j, 0)
                done(pe, s_added, g, j, 2)
                for k in range(TILES):
                    ins = nc.tensor.matmul(sum_ps[:, j % 2, 0:F + 1], hot_f[:, j % 2, k, :], msg[:, j % 2, k, :],
                                           start=k == 0, stop=k == TILES - 1)
                ins.then_inc(s_sum[j], 1)

            def windows(g):
                pe.wait_ge(win_tab, g * 16 + 16)
                pe.sem_inc(passed, 1)
                w = [pe.value_load(wins[:, SLOTS - 1 + j:SLOTS + j], min_val=0, max_val=max_w) for j in range(SLOTS)]
                pe.sem_inc(pe_has, 1)
                return w

            def back(g, j, lag):
                if j >= lag:
                    return g, j - lag
                return None if isinstance(g, int) and g == 0 else (g + (-1), j - lag + SLOTS)

            def one(g):
                w = windows(g)
                for j in range(SLOTS):
                    turn(g, j)
                    if b := back(g, j, 1):
                        product(*b, w[j])
                    if b := back(g, j, 3):
                        window_sum(*b)

            def drain(g):
                w = pe.value_load(wins[:, 2 * SLOTS - 1:2 * SLOTS], min_val=0, max_val=max_w)
                product(*back(g, 0, 1), w)
                for j in range(3):
                    window_sum(*back(g, j, 3))
            turns(pe, groups, one, drain)

        @block.scalar
        def _(act):
            groups = n_groups(act)

            def copy_turned(g, j):
                done(act, s_turn, g, j, 0)
                done(act, s_prod, g, j, 2)
                nc.scalar.copy(hot_t[:, j % 2], turn_ps[:, j % 2, 0:TILES * P].rearrange("p (k n) -> p k n", k=TILES)
                               ).then_inc(s_hot_t[j], 1)

            def soft_parts(g, j):
                done(act, s_abs, g, j, 0)
                done(act, s_logs, g, j, 2)
                nc.scalar.activation(expo[:, j % 2], pre[:, j % 2], ACT.Exp, scale=-1.0).then_inc(s_expo[j], 1)
                done(act, s_expo, g, j, 0)
                done(act, s_soft, g, j, 2)
                done(act, s_gate, g, j, 2)
                nc.scalar.activation(logs[:, j % 2], expo[:, j % 2], ACT.Ln, bias=1.0).then_inc(s_logs[j], 1)
                done(act, s_sum, g, j, 2)
                nc.scalar.copy(hot_f[:, j % 2], hot[:, j]).then_inc(s_hot_f[j], 1)
                done(act, s_logs, g, j, 0)
                done(act, s_msg, g, j, 2)
                nc.scalar.activation(gate[:, j % 2], logs[:, j % 2, :, 0:F], ACT.Exp, scale=-1.0).then_inc(s_gate[j], 1)

            def back(g, j, lag):
                if j >= lag:
                    return g, j - lag
                return None if isinstance(g, int) and g == 0 else (g + (-1), j - lag + SLOTS)

            def one(g):
                for j in range(SLOTS):
                    copy_turned(g, j)
                    if b := back(g, j, 2):
                        soft_parts(*b)

            def drain(g):
                for j in range(2):
                    soft_parts(*back(g, j, 2))
            turns(act, groups, one, drain)

        @block.vector
        def _(v):
            nc.vector.memset(t["sums"][:], 0.0).then_inc(ready, 1)
            groups = n_groups(v)
            v.wait_ge(ready, 2)

            def one_hot(g, j, win):
                done(v, ends_in, g, j, 0, 16)
                done(v, s_turn, g, j, SLOTS)
                done(v, s_hot_f, g, j, SLOTS)
                for k in range(TILES):
                    ins = nc.vector.tensor_scalar(hot[:, j, k, :], t["node_no"][:, bass.ds(win * P, P)],
                                                  ends[:, j, k, 1:2], None, ALU.is_equal)
                ins.then_inc(s_hot[j], 1)

            def sums(g, j):
                done(v, s_prod, g, j, 0)
                done(v, src_in, g, j, 0, 32)
                done(v, s_expo, g, j, 2)
                done(v, s_abs, g, j, 2)
                done(v, s_soft, g, j, 2)
                nc.vector.tensor_tensor(pre[:, j % 2], pre_ps[:, j % 2], from_src[:, j], ALU.add).then_inc(s_pre[j], 1)

            def magnitude(g, j):
                done(v, s_pre, g, j, 0)
                nc.vector.tensor_scalar(value[:, j % 2], pre[:, j % 2, :, F:F2], 0.0, None, ALU.max)
                nc.vector.scalar_tensor_tensor(pre[:, j % 2, :, F:F2], pre[:, j % 2, :, F:F2], -1.0,
                                               pre[:, j % 2, :, F:F2], ALU.mult, ALU.max).then_inc(s_abs[j], 1)

            def softplus(g, j):
                done(v, s_logs, g, j, 0)
                done(v, s_abs, g, j, 0)
                done(v, s_msg, g, j, 2)
                nc.vector.tensor_tensor(soft[:, j % 2], value[:, j % 2], logs[:, j % 2, :, F:F2], ALU.add
                                        ).then_inc(s_soft[j], 1)

            def message(g, j):
                done(v, s_soft, g, j, 0)
                done(v, s_gate, g, j, 0)
                done(v, s_sum, g, j, 2)
                nc.vector.tensor_tensor(msg[:, j % 2, :, 0:F], soft[:, j % 2], gate[:, j % 2], ALU.mult
                                        ).then_inc(s_msg[j], 1)

            def add_up(g, j, win):
                done(v, s_sum, g, j, 0)
                done(v, s_added, g, j, 1)
                rows = t["sums"][:, bass.ds(win * (F + 1), F + 1)]
                nc.vector.tensor_tensor(rows, sum_ps[:, j % 2, 0:F + 1], rows, ALU.add).then_inc(s_added[j], 1)

            def back(g, j, lag):
                if j >= lag:
                    return g, j - lag
                return None if isinstance(g, int) and g == 0 else (g + (-1), j - lag + SLOTS)

            def load_windows(first, n):
                return [v.value_load(wins[:, first + j:first + j + 1], min_val=0, max_val=max_w) for j in range(n)]

            def one(g):
                v.wait_ge(win_tab, g * 16 + 16)
                v.sem_inc(passed, 1)
                w = load_windows(0, 2 * SLOTS)
                v.sem_inc(dve_has, 1)
                for j in range(SLOTS):
                    one_hot(g, j, w[SLOTS + j])
                    if b := back(g, j, 2):
                        sums(*b)
                    if b := back(g, j, 3):
                        softplus(*b)
                    if b := back(g, j, 2):
                        magnitude(*b)
                    if b := back(g, j, 3):
                        message(*b)
                    if b := back(g, j, 4):
                        add_up(*b, w[j])

            def drain(g):
                w = load_windows(SLOTS, SLOTS)
                for j in range(SLOTS):
                    if j < 2:
                        sums(*back(g, j, 2))
                        magnitude(*back(g, j, 2))
                    if j < 3:
                        softplus(*back(g, j, 3))
                        message(*back(g, j, 3))
                    add_up(*back(g, j, 4), w[j])
                v.wait_ge(s_added[SLOTS - 1], g)
                v.sem_inc(passed, 1)
            turns(v, groups, one, drain)


def set_up(nc, t, d):
    with nc.cleanup_on_exit(), ExitStack() as ctx:
        sem = lambda name: nc.alloc_semaphore(name)
        vec = ctx.enter_context(nc.sbuf_tensor("bn_vec", [P, 2, 4, F], F32))
        root = ctx.enter_context(nc.sbuf_tensor("bn_root", [P, 2, F], F32))
        inv = ctx.enter_context(nc.sbuf_tensor("bn_inv", [P, 2, F], F32))
        loaded, nodes_in, filled, rooted, chain = (sem(n) for n in (
            "bn_in", "nodes_in", "filled", "rooted", "bn_chain"))
        block = ctx.enter_context(nc.Block())

        @block.sync
        def _(sp):
            for layer in (1, 2):
                for k, name in enumerate(("gamma", "beta", "rmean", "rvar")):
                    sp.dma_start(vec[:, layer - 1, k, :], d[f"W{layer}"][name].rearrange("(a f) -> a f", a=1)
                                 .to_broadcast([P, F])).then_inc(loaded, 16)
            sp.dma_start(t["x_nodes"][:].rearrange("p (w f) -> p w f", f=F),
                         d["x"].rearrange("(w p) f -> p w f", p=P)).then_inc(nodes_in, 16)

        @block.gpsimd
        def _(pool):
            for name in ("ident", "ident_b"):
                nc.gpsimd.memset(t[name][:], 0.0).then_inc(filled, 1)
            for n, name in enumerate(("ident", "ident_b")):
                pool.wait_ge(filled, 2 + n)
                nc.gpsimd.affine_select(out=t[name][:], in_=t[name][:], compare_op=ALU.not_equal, fill=1.0, base=0,
                                        pattern=[[-1, P]], channel_multiplier=1).then_inc(filled, 1)
            pool.wait_ge(filled, 4)

        @block.scalar
        def _(act):
            act.wait_ge(chain, 1)
            nc.scalar.activation(root[:], vec[:, :, 3, :], ACT.Sqrt).then_inc(rooted, 1)

        @block.vector
        def _(v):
            n = [0]

            def after(ins):
                n[0] += 1
                ins.then_inc(chain, 1)
                v.wait_ge(chain, n[0])

            v.wait_ge(loaded, 16 * 8)
            after(nc.vector.tensor_scalar(vec[:, :, 3, :], vec[:, :, 3, :], BN_EPS, None, ALU.add))
            v.wait_ge(rooted, 1)
            after(nc.vector.reciprocal(inv[:], root[:]))
            v.wait_ge(nodes_in, 16)
            for k in range(2):
                scale, shift = t[f"bn_scale{k + 1}"], t[f"bn_shift{k + 1}"]
                after(nc.vector.tensor_tensor(scale[:], inv[:, k, :], vec[:, k, 0, :], ALU.mult))
                after(nc.vector.tensor_tensor(shift[:], vec[:, k, 2, :], scale[:], ALU.mult))
                after(nc.vector.tensor_tensor(shift[:], vec[:, k, 1, :], shift[:], ALU.subtract))
            nodes = t["x_nodes"][:].rearrange("p (w f) -> p w f", f=F)
            after(nc.vector.tensor_tensor(nodes, nodes, t["bn_shift1"][:].unsqueeze(1).to_broadcast([P, WPAD, F]),
                                          ALU.add))


def inverse_counts(nc, t, layer):
    with nc.cleanup_on_exit(), ExitStack() as ctx:
        s = nc.alloc_semaphore(f"count_chain{layer}")
        block = ctx.enter_context(nc.Block())

        @block.vector
        def _(v):
            counts = t["sums"][:].rearrange("p (w f) -> p w f", f=F + 1)[:, :, F]
            nc.vector.tensor_scalar(t["per_count"][:, 0:WPAD], counts, 1.0, None, ALU.max).then_inc(s, 1)
            v.wait_ge(s, 1)
            nc.vector.reciprocal(t["per_count"][:, 0:WPAD], t["per_count"][:, 0:WPAD]).then_inc(s, 1)
            v.wait_ge(s, 2)


def finish(nc, t, d, out):
    with nc.cleanup_on_exit(), ExitStack() as ctx:
        sem = lambda name: nc.alloc_semaphore(name)
        sb = lambda name, shape: ctx.enter_context(nc.sbuf_tensor(name, shape, F32))
        mean, var, eps = sb("mean", [P, WINDOWS]), sb("var", [P, WINDOWS]), sb("ln_eps", [P, 1])
        x_again, chain, squared, rooted, stored = (sem(n) for n in (
            "x_again", "ln_chain", "squared", "ln_rooted", "stored"))
        wide = lambda a: a.unsqueeze(2).to_broadcast([P, WINDOWS, F])
        x0 = t["node_no"][:].rearrange("p (w f) -> p w f", f=F)
        y = t["x_nodes"][:].rearrange("p (w f) -> p w f", f=F)[:, 0:WINDOWS, :]
        sums = t["sums"][:].rearrange("p (w f) -> p w f", f=F + 1)[:, 0:WINDOWS, 0:F]
        whole = NODES // P
        left = NODES - whole * P
        block = ctx.enter_context(nc.Block())

        @block.sync
        def _(sp):
            sp.dma_start(x0, d["x"][0:WINDOWS * P, :].rearrange("(w p) f -> p w f", p=P)).then_inc(x_again, 16)
            sp.wait_ge(chain, 12)
            sp.dma_start(out[0:whole * P, :].rearrange("(w p) f -> p w f", p=P), y[:, 0:whole, :]).then_inc(stored, 16)
            sp.dma_start(out[whole * P:NODES, :], y[0:left, whole, :]).then_inc(stored, 16)
            sp.wait_ge(stored, 32)

        @block.scalar
        def _(act):
            act.wait_ge(chain, 8)
            nc.scalar.activation(sums, y, ACT.Square).then_inc(squared, 1)
            act.wait_ge(chain, 10)
            nc.scalar.activation(var[:], var[:], ACT.Sqrt).then_inc(rooted, 1)

        @block.vector
        def _(v):
            n = [0]

            def after(ins):
                n[0] += 1
                ins.then_inc(chain, 1)
                v.wait_ge(chain, n[0])

            tt = nc.vector.tensor_tensor
            after(tt(sums, sums, wide(t["per_count"][:, 0:WINDOWS]), ALU.mult))
            after(tt(sums, sums, t["bn_scale2"][:].unsqueeze(1).to_broadcast([P, WINDOWS, F]), ALU.mult))
            after(tt(y, y, sums, ALU.add))
            after(tt(y, y, t["bn_shift2"][:].unsqueeze(1).to_broadcast([P, WINDOWS, F]), ALU.add))
            v.wait_ge(x_again, 16)
            after(tt(y, y, x0, ALU.add))
            after(nc.vector.tensor_reduce(mean[:], y, AX.X, ALU.add))
            after(nc.vector.tensor_scalar(mean[:], mean[:], 1.0 / F, None, ALU.mult))
            after(tt(y, y, wide(mean[:]), ALU.subtract))
            v.wait_ge(squared, 1)
            after(nc.vector.tensor_reduce(var[:], sums, AX.X, ALU.add))
            after(nc.vector.tensor_scalar(var[:], var[:], 1.0 / F, LN_EPS, ALU.mult, ALU.add))
            v.wait_ge(rooted, 1)
            after(nc.vector.reciprocal(var[:], var[:]))
            after(tt(y, y, wide(var[:]), ALU.mult))


def graph_layers(nc, d, out):
    with ExitStack() as ctx:
        sb = lambda name, shape, dt: ctx.enter_context(nc.sbuf_tensor(name, shape, dt))
        ctx.enter_context(nc.allow_non_contiguous_dma(reason="16-byte rows of edge ends, and small tables"))
        t = {
            "off_dram": nc.dram_tensor("off_table", [TABLE], I32, kind="Internal").ap(),
            "win_dram": nc.dram_tensor("win_table", [TABLE], I32, kind="Internal").ap(),
            "src_dram1": nc.dram_tensor("src_rows1", [NPAD, F2], F32, kind="Internal").ap(),
            "src_dram2": nc.dram_tensor("src_rows2", [NPAD, F2], F32, kind="Internal").ap(),
            "choice": sb("choice", [1, 2], I32),
            "node_no": sb("node_no", [P, WINDOWS * P], F32),
            "sums": sb("sums", [P, WPAD * (F + 1)], F32),
            "per_count": sb("per_count", [P, WPAD], F32),
            "ident": sb("ident", [P, P], F32),
            "ident_b": sb("ident_b", [P, P], BF16),
            "bn_scale1": sb("bn_scale1", [P, F], F32), "bn_shift1": sb("bn_shift1", [P, F], F32),
            "bn_scale2": sb("bn_scale2", [P, F], F32), "bn_shift2": sb("bn_shift2", [P, F], F32),
        }
        plan_steps(nc, t, d)
        t["x_nodes"] = sb("x_nodes", [P, WPAD * F], F32)
        t["dst_parts"] = sb("dst_parts", [P, WPAD * 3 * F2], BF16)
        set_up(nc, t, d)
        layer_tables(nc, t, d, 1)
        edge_loop(nc, t, d, 1)
        inverse_counts(nc, t, 1)
        layer_tables(nc, t, d, 2)
        edge_loop(nc, t, d, 2)
        finish(nc, t, d, out)


def kernel(**inputs):
    import concourse.bacc as bacc
    from concourse.bass_utils import run_bass_kernel_spmd

    a = {k: np.asarray(v) for k, v in inputs.items()}
    nc = bacc.Bacc("TRN2", target_bir_lowering=False, num_devices=1)
    arrays = {}

    def given(name, array):
        array = np.ascontiguousarray(array)
        arrays[name] = array
        return nc.dram_tensor(name, array.shape, mybir.dt.from_np(array.dtype), kind="ExternalInput").ap()

    x = np.zeros((NPAD, F), a["x"].dtype)
    x[:NODES] = a["x"]
    ends = np.zeros((EPAD, 2), a["src"].dtype)
    ends[:, 1] = NO_WINDOW
    ends[:EDGES, 0] = a["src"]
    ends[:EDGES, 1] = a["dst"]
    dst = np.full((EPAD + P,), NO_WINDOW, a["dst"].dtype)
    dst[:EDGES] = a["dst"]
    edge_t = np.zeros((FE, EPAD), a["edge_attr_64"].dtype)
    edge_t[:, :EDGES] = a["edge_attr_64"].T
    d = {
        "x": given("x_rows", x), "xT": given("x_cols", x.T), "ends": given("edge_ends", ends),
        "dst": given("destinations", dst), "edge_t": given("edge_cols", edge_t),
    }
    for layer in (1, 2):
        p = {k: a[f"L0_gnn_{k}{layer}"] for k in ("Wf", "bf", "Ws", "bs", "gamma", "beta", "rmean", "rvar")}
        both = np.concatenate([p["Wf"], p["Ws"]], axis=1)
        d[f"W{layer}"] = {
            "node": given(f"in_w_node{layer}", np.concatenate([both[:F], both[F:2 * F]], axis=1)),
            "edge": given(f"in_w_edge{layer}", both[2 * F:]),
            "bias": given(f"in_bias{layer}", np.concatenate([p["bf"], p["bs"]])),
            **{k: given(f"{k}{layer}", p[k]) for k in ("gamma", "beta", "rmean", "rvar")},
        }
    out = nc.dram_tensor("out", (NODES, F), F32, kind="ExternalOutput").ap()
    graph_layers(nc, d, out)
    r = run_bass_kernel_spmd(nc, [arrays], core_ids=[0])
    return r.results[0]["out"]
```

```python
from contextlib import ExitStack

import numpy as np

import concourse.bass as bass
from concourse import mybir

ALU = mybir.AluOpType
ACT = mybir.ActivationFunctionType
AX = mybir.AxisListType
F32 = mybir.dt.float32
BF16 = mybir.dt.bfloat16
I32 = mybir.dt.int32
U32 = mybir.dt.uint32

P = 128
NODES = 6250
EDGES = 100000
F = 128
FE = 64
F2 = 2 * F
BN_EPS = 1e-5
LN_EPS = 1e-5

WINDOWS = -(-NODES // P)
WPAD = WINDOWS + WINDOWS % 2
NPAD = WPAD * P
TILES = 2
STEP = TILES * P
SLOTS = 4
EPAD = -(-(EDGES + STEP) // P) * P
NO_WINDOW = NPAD + 1024
ECOLS = EPAD // P
SORTED_GROUPS = -(-((EDGES + WINDOWS * (STEP - 1)) // STEP) // SLOTS)
SORTED_STEPS = SORTED_GROUPS * SLOTS
SCOLS = -(-SORTED_STEPS // P)
BLOCKS = -(-EDGES // STEP)
GENERAL_GROUPS = -(-(BLOCKS * WINDOWS) // SLOTS)
GENERAL_STEPS = GENERAL_GROUPS * SLOTS
BEFORE = 2 * SLOTS
SORTED_AT = BEFORE
GENERAL_AT = SORTED_AT + SCOLS * P + BEFORE
TABLE = GENERAL_AT + GENERAL_STEPS + SLOTS


def plan_steps(nc, t, d):
    with nc.cleanup_on_exit(), ExitStack() as ctx:
        sb = lambda name, shape, dt: ctx.enter_context(nc.sbuf_tensor(name, shape, dt))
        sem = lambda name: nc.alloc_semaphore(name)
        dst_i = sb("dst_i", [P, 2, ECOLS], I32)
        dst_f = sb("dst_f", [P, 2, ECOLS], F32)
        below = sb("below", [P, ECOLS], F32)
        counts = sb("counts", [P, WINDOWS + 1], F32)
        ones = sb("ones", [P, P], F32)
        total = sb("total", [P, WINDOWS + 1], F32)
        in_window = sb("in_window", [P, WINDOWS], F32)
        steps_i = sb("steps_i", [P, WINDOWS], I32)
        steps_f = sb("steps_f", [P, WINDOWS], F32)
        step_end = sb("step_end", [P, WINDOWS], F32)
        shift = sb("shift", [P, WINDOWS], F32)
        step_no = sb("step_no", [P, SCOLS], F32)
        passed = sb("passed", [P, SCOLS, WINDOWS], F32)
        shifted = sb("shifted", [P, SCOLS, WINDOWS], F32)
        win_f = sb("win_f", [P, SCOLS], F32)
        off_f = sb("off_f", [P, SCOLS], F32)
        entry = sb("entry", [P, 2, SCOLS], I32)
        flag_f = sb("flag_f", [1, 4], F32)
        gen_off = sb("gen_off", [WINDOWS, BLOCKS], I32)
        gen_win = sb("gen_win", [WINDOWS, BLOCKS], I32)
        tail = sb("tail", [1, 2, BEFORE], I32)
        total_ps = ctx.enter_context(nc.psum_tensor("total_ps", [P, 512], F32))

        dst_in = sem("dst_in")
        iotas = sem("iotas")
        dve = sem("dve_done")
        summed = sem("summed")
        written = sem("written")
        general = t["off_dram"][GENERAL_AT:GENERAL_AT + WINDOWS * BLOCKS].rearrange("(w k) -> w k", k=BLOCKS)
        general_w = t["win_dram"][GENERAL_AT:GENERAL_AT + WINDOWS * BLOCKS].rearrange("(w k) -> w k", k=BLOCKS)
        rest = TABLE - GENERAL_AT - WINDOWS * BLOCKS
        sorted_off = t["off_dram"][SORTED_AT:SORTED_AT + SCOLS * P].rearrange("(p c) -> p c", c=SCOLS)
        sorted_win = t["win_dram"][SORTED_AT:SORTED_AT + SCOLS * P].rearrange("(p c) -> p c", c=SCOLS)

        block = ctx.enter_context(nc.Block())

        @block.sync
        def _(sp):
            sp.dma_start(dst_i[:, 0, :], d["dst"][0:EPAD].rearrange("(p c) -> p c", c=ECOLS)).then_inc(dst_in, 16)
            sp.dma_start(dst_i[:, 1, :], d["dst"][1:EPAD + 1].rearrange("(p c) -> p c", c=ECOLS)).then_inc(dst_in, 16)
            sp.wait_ge(iotas, 5)
            sp.dma_start(general, gen_off[:]).then_inc(written, 16)
            sp.dma_start(general_w, gen_win[:]).then_inc(written, 16)
            n = 2
            for table, k in ((t["off_dram"], 0), (t["win_dram"], 1)):
                for at, many in ((0, BEFORE), (GENERAL_AT - BEFORE, BEFORE), (TABLE - rest, rest)):
                    if many:
                        sp.dma_start(table[at:at + many].rearrange("(a c) -> a c", a=1),
                                     tail[:, k, 0:many]).then_inc(written, 16)
                        n += 1
            sp.wait_ge(dve, 1)
            sp.dma_start(sorted_off, entry[:, 0, :]).then_inc(written, 16)
            sp.dma_start(sorted_win, entry[:, 1, :]).then_inc(written, 16)
            sp.wait_ge(written, 16 * (n + 2))

        @block.gpsimd
        def _(pool):
            nc.gpsimd.iota(step_no[:], [[1, SCOLS]], base=0, channel_multiplier=SCOLS,
                           allow_small_or_imprecise_dtypes=True).then_inc(iotas, 1)
            nc.gpsimd.iota(gen_off[:], [[STEP, BLOCKS]], base=0, channel_multiplier=0).then_inc(iotas, 1)
            nc.gpsimd.iota(gen_win[:], [[0, BLOCKS]], base=0, channel_multiplier=1).then_inc(iotas, 1)
            nc.gpsimd.iota(tail[:, 0, :], [[0, BEFORE]], base=EDGES, channel_multiplier=0).then_inc(iotas, 1)
            nc.gpsimd.iota(tail[:, 1, :], [[0, BEFORE]], base=WINDOWS - 1, channel_multiplier=0).then_inc(iotas, 1)
            nc.gpsimd.iota(t["node_no"][:], [[1, WINDOWS * P]], base=0, channel_multiplier=0,
                           allow_small_or_imprecise_dtypes=True).then_inc(iotas, 1)

        @block.tensor
        def _(pe):
            pe.wait_ge(summed, 1)
            nc.tensor.matmul(total_ps[:, 0:WINDOWS + 1], ones[:], counts[:], start=True, stop=True).then_inc(summed, 1)

        @block.vector
        def _(v):
            own = sem("plan_chain")
            n = [0]

            def after(ins):
                n[0] += 1
                ins.then_inc(own, 1)
                v.wait_ge(own, n[0])

            nc.vector.memset(ones[:], 1.0)
            v.wait_ge(dst_in, 32)
            after(nc.vector.tensor_copy(dst_f[:], dst_i[:]))
            after(nc.vector.tensor_tensor(below[:], dst_f[:, 0, :], dst_f[:, 1, :], ALU.is_gt))
            after(nc.vector.tensor_reduce(counts[:, WINDOWS:WINDOWS + 1], below[:], AX.X, ALU.add))
            for w in range(WINDOWS):
                last = nc.vector.tensor_scalar(below[:], dst_f[:, 0, :], float(P * (w + 1)), None, ALU.is_lt,
                                               ALU.add, accum_out=counts[:, w:w + 1])
                after(last)
            v.sem_inc(summed, 1)
            v.wait_ge(summed, 2)
            after(nc.vector.tensor_copy(total[:], total_ps[:, 0:WINDOWS + 1]))
            nc.vector.tensor_copy(in_window[:, 0:1], total[:, 0:1])
            after(nc.vector.tensor_tensor(in_window[:, 1:], total[:, 1:WINDOWS], total[:, 0:WINDOWS - 1], ALU.subtract))
            after(nc.vector.tensor_scalar(steps_i[:], in_window[:], float(STEP - 1), None, ALU.add))
            after(nc.vector.tensor_scalar(steps_i[:], steps_i[:], STEP.bit_length() - 1, None, ALU.arith_shift_right))
            after(nc.vector.tensor_copy(steps_f[:], steps_i[:]))
            after(nc.vector.tensor_tensor_scan(step_end[:], steps_f[:], steps_f[:], 0.0, ALU.add, ALU.bypass))
            after(nc.vector.scalar_tensor_tensor(shift[:], steps_f[:], -float(STEP), in_window[:], ALU.mult, ALU.add))
            v.wait_ge(iotas, 6)
            for c in range(SCOLS):
                after(nc.vector.tensor_scalar(passed[:, c, :], step_end[:], step_no[:, c:c + 1], None, ALU.is_le))
                after(nc.vector.tensor_tensor(shifted[:, c, :], passed[:, c, :], shift[:], ALU.mult))
            after(nc.vector.tensor_reduce(win_f[:], passed[:], AX.X, ALU.add))
            after(nc.vector.tensor_reduce(off_f[:], shifted[:], AX.X, ALU.add))
            after(nc.vector.scalar_tensor_tensor(off_f[:], step_no[:], float(STEP), off_f[:], ALU.mult, ALU.add))
            after(nc.vector.tensor_scalar(entry[:, 0, :], off_f[:], float(EDGES), None, ALU.min))
            after(nc.vector.tensor_scalar(flag_f[:, 0:1], total[0:1, WINDOWS:WINDOWS + 1], 1.0, None, ALU.min))
            after(nc.vector.tensor_scalar(t["choice"][:, 0:1], flag_f[:, 0:1], float(GENERAL_GROUPS - SORTED_GROUPS),
                                          float(SORTED_GROUPS - 2), ALU.mult, ALU.add))
            after(nc.vector.tensor_scalar(t["choice"][:, 1:2], flag_f[:, 0:1], float(GENERAL_AT - SORTED_AT),
                                          None, ALU.mult))
            nc.vector.tensor_scalar(entry[:, 1, :], win_f[:], float(WINDOWS - 1), None, ALU.min).then_inc(dve, 1)
            v.wait_ge(dve, 1)


def layer_tables(nc, t, d, layer):
    with nc.cleanup_on_exit(), ExitStack() as ctx:
        sb = lambda name, shape, dt: ctx.enter_context(nc.sbuf_tensor(f"{name}{layer}", shape, dt))
        sem = lambda name: nc.alloc_semaphore(f"{name}{layer}")
        ps = lambda name, shape, dt: ctx.enter_context(nc.psum_tensor(f"{name}{layer}", shape, dt))
        second = layer == 2
        w_node = sb("w_node", [P, 2 * F2], F32)
        bias = sb("bias", [P, F2], F32)
        x_t = sb("x_t", [P, 2, P], F32)
        dst_part = sb("dst_part", [P, 2, F2], F32)
        rest = sb("rest", [P, 2, F2], F32)
        src_part = sb("src_part", [P, 2, F2], F32)
        scaled = sb("scaled", [P, 2, F], F32)
        x_new = sb("x_new", [P, 2, F], F32)
        dst_ps = ps("dst_ps", [P, 2, 512], F32)
        src_ps = ps("src_ps", [P, 2, 512], F32)
        turned = ps("turned", [P, 2, 512], F32)

        loaded = sem("weights_in")
        x_in = [sem(f"x_in{s}") for s in range(2)]
        x_ready = sem("x_ready")
        x_turned = sem("x_turned")
        x_scaled = sem("x_scaled")
        x_kept = sem("x_kept")
        prod_done = sem("prod_done")
        dst_done = sem("dst_done")
        part1 = sem("part1")
        rest1 = sem("rest1")
        part2 = sem("part2")
        part3 = sem("part3")
        src_done = sem("src_done")
        src_out = [sem(f"src_out{s}") for s in range(2)]
        W, parts, win3 = d[f"W{layer}"], t["dst_parts"], 3 * F2
        PAIRS = WPAD // 2

        block = ctx.enter_context(nc.Block())

        def windows(eng, step):
            for s in range(2):
                step(s, 0, s, True)
            with eng.Fori(1, PAIRS) as q:
                for s in range(2):
                    step(q * 2 + s, q, s, False)

        @block.sync
        def _(sp):
            sp.dma_start(w_node[:], W["node"]).then_inc(loaded, 16)
            sp.dma_start(bias[:], W["bias"].rearrange("(a f) -> a f", a=1).to_broadcast([P, F2])).then_inc(loaded, 16)

            def step(w, q, s, first):
                if not second:
                    if not first:
                        sp.wait_ge(prod_done, q * 2 + (s - 1))
                    sp.dma_start(x_t[:, s, :], d["xT"][:, bass.ds(w * P, P)]).then_inc(x_in[s], 16)
            if not second:
                windows(sp, step)

        @block.gpsimd
        def _(pool):
            def step(w, q, s, first):
                pool.wait_ge(src_done, q * 2 + (s + 1))
                pool.dma_start(t[f"src_dram{layer}"][bass.ds(w * P, P), :], src_part[:, s, :]).then_inc(src_out[s], 16)
            windows(pool, step)
            for s in range(2):
                pool.wait_ge(src_out[s], 16 * PAIRS)

        @block.tensor
        def _(pe):
            pe.wait_ge(loaded, 32)

            def step(w, q, s, first):
                if second:
                    pe.wait_ge(x_scaled, q * 2 + (s + 1))
                    nc.tensor.transpose(turned[:, s, 0:P], x_new[:, s, :], t["ident"][:]).then_inc(x_turned, 1)
                    pe.wait_ge(x_ready, q * 2 + (s + 1))
                else:
                    pe.wait_ge(x_in[s], q * 16 + 16)
                if not first:
                    pe.wait_ge(dst_done, q * 2 + (s - 1))
                    pe.wait_ge(src_done, q * 2 + (s - 1))
                nc.tensor.matmul(dst_ps[:, s, 0:F2], x_t[:, s, :], w_node[:, 0:F2], start=True, stop=True)
                nc.tensor.matmul(src_ps[:, s, 0:F2], x_t[:, s, :], w_node[:, F2:2 * F2], start=True, stop=True
                                 ).then_inc(prod_done, 1)
            windows(pe, step)

        @block.scalar
        def _(act):
            def step(w, q, s, first):
                if second:
                    act.wait_ge(x_turned, q * 2 + (s + 1))
                    if not first:
                        act.wait_ge(prod_done, q * 2 + (s - 1))
                    nc.scalar.copy(x_t[:, s, :], turned[:, s, 0:P]).then_inc(x_ready, 1)
                    nc.scalar.copy(t["x_nodes"][:, bass.ds(w * F, F)], x_new[:, s, :]).then_inc(x_kept, 1)
                act.wait_ge(prod_done, q * 2 + (s + 1))
                if not first:
                    act.wait_ge(src_out[s], q * 16)
                nc.scalar.copy(src_part[:, s, :], src_ps[:, s, 0:F2]).then_inc(src_done, 1)
                act.wait_ge(dst_done, q * 2 + (s + 1))
                nc.scalar.copy(parts[:, bass.ds(w * win3, F2)], dst_part[:, s, :]).then_inc(part1, 1)
                act.wait_ge(rest1, q * 2 + (s + 1))
                nc.scalar.copy(parts[:, bass.ds(w * win3 + F2, F2)], rest[:, s, :]).then_inc(part2, 1)
            windows(act, step)

        @block.vector
        def _(v):
            v.wait_ge(loaded, 32)

            def step(w, q, s, first):
                if second:
                    if not first:
                        v.wait_ge(x_turned, q * 2 + (s - 1))
                        v.wait_ge(x_kept, q * 2 + (s - 1))
                    nc.vector.scalar_tensor_tensor(
                        scaled[:, s, :], t["sums"][:, bass.ds(w * (F + 1), F)], t["per_count"][:, bass.ds(w, 1)],
                        t["bn_scale1"][:], ALU.mult, ALU.mult).then_inc(own, 1)
                    v.wait_ge(own, q * 2 + (s + 1))
                    nc.vector.tensor_tensor(x_new[:, s, :], t["x_nodes"][:, bass.ds(w * F, F)], scaled[:, s, :],
                                            ALU.add).then_inc(x_scaled, 1)
                v.wait_ge(prod_done, q * 2 + (s + 1))
                if not first:
                    v.wait_ge(part3, q * 2 + (s - 1))
                nc.vector.tensor_tensor(dst_part[:, s, :], dst_ps[:, s, 0:F2], bias[:], ALU.add).then_inc(dst_done, 1)
                v.wait_ge(part1, q * 2 + (s + 1))
                nc.vector.tensor_tensor(rest[:, s, :], dst_part[:, s, :], parts[:, bass.ds(w * win3, F2)],
                                        ALU.subtract).then_inc(rest1, 1)
                v.wait_ge(part2, q * 2 + (s + 1))
                nc.vector.tensor_tensor(parts[:, bass.ds(w * win3 + 2 * F2, F2)], rest[:, s, :],
                                        parts[:, bass.ds(w * win3 + F2, F2)], ALU.subtract).then_inc(part3, 1)
            own = sem("scaled")
            windows(v, step)


def edge_loop(nc, t, d, layer):
    with nc.cleanup_on_exit(), ExitStack() as ctx:
        sb = lambda name, shape, dt: ctx.enter_context(nc.sbuf_tensor(f"{name}{layer}", shape, dt))
        ps = lambda name, shape, dt: ctx.enter_context(nc.psum_tensor(f"{name}{layer}", shape, dt))
        sem = lambda name: nc.alloc_semaphore(f"{name}{layer}")
        each = lambda name: [nc.alloc_semaphore(f"{name}{layer}_{j}") for j in range(SLOTS)]

        w_edge = sb("w_edge", [FE, F2], F32)
        sp_off = sb("sp_off", [1, SLOTS + 1], I32)
        wins = sb("wins", [1, BEFORE + SLOTS], I32)
        ends = sb("ends", [P, SLOTS, TILES, 2], I32)
        edge_t = sb("edge_t", [FE, SLOTS, STEP], F32)
        from_src = sb("from_src", [P, SLOTS, TILES, F2], F32)
        hot = sb("hot", [P, SLOTS, TILES, P], BF16)
        hot_t = sb("hot_t", [P, 2, TILES, P], BF16)
        hot_f = sb("hot_f", [P, 2, TILES, P], F32)
        pre = sb("pre", [P, SLOTS, TILES, F2], F32)
        size = sb("size", [P, 2, TILES, F], F32)
        logs = sb("logs", [P, SLOTS, TILES, F2], F32)
        msg = sb("msg", [P, 2, TILES, F + 1], F32)
        turn_ps = ps("turn_ps", [P, 2, 1024], BF16)
        pre_ps = ps("pre_ps", [P, 2, TILES, F2], F32)
        sum_ps = ps("sum_ps", [P, 2, 512], F32)

        w_in = sem("w_edge_in")
        sp_tab = sem("sp_table_in")
        win_tab = sem("windows_in")
        pe_has = sem("pe_has_windows")
        dve_has = sem("dve_has_windows")
        ready = sem("ones_ready")
        passed = sem("waits_passed")
        ends_in, edge_in, src_in = each("ends_in"), each("edge_in"), each("src_in")
        s_hot, s_turn, s_hot_t, s_hot_f = each("hot_done"), each("turn_done"), each("hot_t_done"), each("hot_f_done")
        s_prod, s_pre, s_abs, s_expo = each("prod_done"), each("pre_done"), each("abs_done"), each("expo_done")
        s_logs, s_gate, s_soft, s_msg = each("logs_done"), each("gate_done"), each("soft_done"), each("msg_done")
        s_sum, s_added = each("sum_done"), each("added")

        max_w = WINDOWS - 1
        win3 = 3 * F2
        block = ctx.enter_context(nc.Block())

        def done(eng, sems, g, j, lag, each_inc=1):
            turns_back = (lag - j + SLOTS - 1) // SLOTS if lag > j else 0
            if isinstance(g, int):
                if g < turns_back:
                    return
                eng.wait_ge(sems[(j - lag) % SLOTS], (g - turns_back + 1) * each_inc)
            elif turns_back == 0:
                eng.wait_ge(sems[j - lag], g * each_inc + each_inc)
            else:
                eng.wait_ge(sems[(j - lag) % SLOTS], (g + (1 - turns_back)) * each_inc)

        def back(g, j, lag):
            turns_back = (lag - j + SLOTS - 1) // SLOTS if lag > j else 0
            if isinstance(g, int) and g < turns_back:
                return None
            return (g + (-turns_back) if turns_back else g), (j - lag) % SLOTS

        def turns(eng, groups, one, drain, peeled=1):
            for g in range(peeled):
                one(g)
            with eng.Fori(peeled, groups) as g:
                one(g)
            drain(groups)

        def load_windows(eng, engine, first, n):
            return nc.values_load_multi_w_load_instructions(
                wins[:, first:first + n], engines=[engine], min_val=0, max_val=max_w,
                skip_runtime_bounds_check_because="plan_steps clamps every entry to the last window")[1]

        def n_groups(eng):
            return eng.value_load(t["choice"][:, 0:1], min_val=SORTED_GROUPS - 2, max_val=GENERAL_GROUPS - 2) + 2

        @block.sync
        def _(sp):
            sp.dma_start(w_edge[:], d[f"W{layer}"]["edge"]).then_inc(w_in, 16)
            groups = n_groups(sp)
            at = sp.value_load(t["choice"][:, 1:2], min_val=0, max_val=GENERAL_AT - SORTED_AT)
            row = lambda table, first, n: table[bass.ds(first, n)].rearrange("(a c) -> a c", a=1)

            def offsets(n):
                return nc.values_load_multi_w_load_instructions(
                    sp_off[:, 0:n], engines=[mybir.EngineType.SP], min_val=0, max_val=EDGES,
                    skip_runtime_bounds_check_because="plan_steps clamps every entry to the number of edges")[1]

            def load_ends(j, off):
                sp.dma_start(ends[:, j, :, :], d["ends"][bass.ds(off, STEP), :].rearrange(
                    "(p k) c -> p k c", k=TILES)).then_inc(ends_in[j], 16)

            def load_edges(j, off):
                sp.dma_start(edge_t[:, j, :], d["edge_t"][:, bass.ds(off, STEP)]).then_inc(edge_in[j], 16)

            sp.dma_start(sp_off[:, 0:SLOTS], row(t["off_dram"], at + SORTED_AT, SLOTS)).then_inc(sp_tab, 16)
            sp.dma_start(wins[:], row(t["win_dram"], at, BEFORE + SLOTS)).then_inc(win_tab, 16)
            sp.wait_ge(sp_tab, 16)
            offs = offsets(SLOTS)
            sp.dma_start(sp_off[:], row(t["off_dram"], at + SORTED_AT + SLOTS - 1, SLOTS + 1)).then_inc(sp_tab, 16)
            for j in range(SLOTS):
                load_ends(j, offs[j])
                if j < SLOTS - 1:
                    load_edges(j, offs[j])

            def one(g):
                sp.wait_ge(sp_tab, g * 16 + 32)
                sp.sem_inc(passed, 1)
                offs = offsets(SLOTS + 1)
                sp.dma_start(sp_off[:], row(t["off_dram"], at + (g + 1) * SLOTS + (SORTED_AT + SLOTS - 1), SLOTS + 1)
                             ).then_inc(sp_tab, 16)
                for j in range(SLOTS):
                    done(sp, s_hot, g, j, 0)
                    sp.sem_inc(passed, 1)
                    done(sp, src_in, g, j, 0, 32)
                    sp.sem_inc(passed, 1)
                    load_ends(j, offs[j + 1])
                    done(sp, s_prod, g, j, 1)
                    sp.sem_inc(passed, 1)
                    load_edges((j - 1) % SLOTS, offs[j])
                    if j == 0:
                        sp.wait_ge(pe_has, g + 1)
                        sp.wait_ge(dve_has, g + 1)
                        sp.sem_inc(passed, 1)
                        sp.dma_start(wins[:], row(t["win_dram"], at + (g + 1) * SLOTS, BEFORE + SLOTS)
                                     ).then_inc(win_tab, 16)

            one(0)
            with sp.Fori(1, groups - 1) as g:
                one(g)
            sp.wait_ge(sp_tab, groups * 16 + 16)
            sp.sem_inc(passed, 1)
            off, = offsets(1)
            sp.wait_ge(s_prod[SLOTS - 2 + 1], groups + (-1))
            sp.sem_inc(passed, 1)
            load_edges(SLOTS - 1, off)

        @block.gpsimd
        def _(pool):
            nc.gpsimd.memset(msg[:, :, :, F:F + 1], 1.0).then_inc(ready, 1)
            groups = n_groups(pool)

            def one(g):
                for j in range(SLOTS):
                    done(pool, ends_in, g, j, 0, 16)
                    done(pool, s_pre, g, j, SLOTS)
                    pool.sem_inc(passed, 1)
                    for k in range(TILES):
                        nc.gpsimd.indirect_dma_start(
                            from_src[:, j, k, :], None, t[f"src_dram{layer}"],
                            bass.IndirectOffsetOnAxis(ap=ends[:, j, k, 0:1], axis=0)).then_inc(src_in[j], 16)
            turns(pool, groups, one, lambda g: None)

        @block.tensor
        def _(pe):
            groups = n_groups(pe)
            pe.wait_ge(w_in, 16)

            def turn(g, j):
                done(pe, s_hot, g, j, 0)
                done(pe, s_hot_t, g, j, 2)
                for k in range(TILES):
                    ins = nc.tensor.transpose(turn_ps[:, j % 2, k * P:(k + 1) * P], hot[:, j, k, :], t["ident_b"][:])
                ins.then_inc(s_turn[j], 1)

            def product(g, j, win):
                done(pe, edge_in, g, j, 0, 16)
                done(pe, s_hot_t, g, j, 0)
                done(pe, s_pre, g, j, 2)
                for k in range(TILES):
                    nc.tensor.matmul(pre_ps[:, j % 2, k, :], edge_t[:, j, k:STEP:TILES], w_edge[:],
                                     start=True, stop=False)
                    for part in range(3):
                        ins = nc.tensor.matmul(pre_ps[:, j % 2, k, :], hot_t[:, j % 2, k, :],
                                               t["dst_parts"][:, bass.ds(win * win3 + part * F2, F2)],
                                               start=False, stop=part == 2)
                ins.then_inc(s_prod[j], 1)

            def window_sum(g, j):
                done(pe, s_hot_f, g, j, 0)
                done(pe, s_msg, g, j, 0)
                done(pe, s_added, g, j, 2)
                for k in range(TILES):
                    ins = nc.tensor.matmul(sum_ps[:, j % 2, 0:F + 1], hot_f[:, j % 2, k, :], msg[:, j % 2, k, :],
                                           start=k == 0, stop=k == TILES - 1)
                ins.then_inc(s_sum[j], 1)

            def one(g):
                pe.wait_ge(win_tab, g * 16 + 16)
                pe.sem_inc(passed, 1)
                w = load_windows(pe, mybir.EngineType.PE, BEFORE - 1, SLOTS)
                pe.sem_inc(pe_has, 1)
                for j in range(SLOTS):
                    turn(g, j)
                    if b := back(g, j, 1):
                        product(*b, w[j])
                    if b := back(g, j, 4):
                        window_sum(*b)

            def drain(g):
                w = load_windows(pe, mybir.EngineType.PE, BEFORE + SLOTS - 1, 1)
                product(*back(g, 0, 1), w[0])
                for j in range(4):
                    window_sum(*back(g, j, 4))
            turns(pe, groups, one, drain)

        @block.scalar
        def _(act):
            nc.scalar.preload_act_table_set("natural_log_exp_and_others")
            groups = n_groups(act)

            def copy_turned(g, j):
                done(act, s_turn, g, j, 0)
                done(act, s_prod, g, j, 2)
                nc.scalar.copy(hot_t[:, j % 2], turn_ps[:, j % 2, 0:TILES * P].rearrange("p (k n) -> p k n", k=TILES)
                               ).then_inc(s_hot_t[j], 1)

            def first_parts(g, j):
                done(act, s_pre, g, j, 0)
                done(act, s_msg, g, j, SLOTS)
                nc.scalar.activation(logs[:, j, :, 0:F], pre[:, j, :, 0:F], ACT.Exp, scale=-1.0)
                done(act, s_abs, g, j, 0)
                nc.scalar.activation(logs[:, j, :, F:F2], size[:, j % 2], ACT.Exp, scale=-1.0).then_inc(s_expo[j], 1)

            def widen(g, j):
                done(act, s_sum, g, j, 2)
                nc.scalar.copy(hot_f[:, j % 2], hot[:, j]).then_inc(s_hot_f[j], 1)

            def second_part(g, j):
                done(act, s_expo, g, j, 0)
                nc.scalar.activation(logs[:, j], logs[:, j], ACT.Ln, bias=1.0).then_inc(s_logs[j], 1)

            def third_part(g, j):
                done(act, s_logs, g, j, 0)
                nc.scalar.activation(logs[:, j, :, 0:F], logs[:, j, :, 0:F], ACT.Exp, scale=-1.0
                                     ).then_inc(s_gate[j], 1)

            def one(g, live=lambda lag, j: True):
                for j in range(SLOTS):
                    if live(0, j):
                        copy_turned(g, j)
                    if live(3, j) and (b := back(g, j, 3)):
                        widen(*b)
                    if live(2, j) and (b := back(g, j, 2)):
                        first_parts(*b)
                    if live(2, j) and (b := back(g, j, 2)):
                        second_part(*b)
                        third_part(*b)

            def drain(g):
                one(g, lambda lag, j: j < lag)
            turns(act, groups, one, drain)

        @block.vector
        def _(v):
            nc.vector.memset(t["sums"][:], 0.0).then_inc(ready, 1)
            groups = n_groups(v)
            v.wait_ge(ready, 2)

            def one_hot(g, j, win):
                done(v, ends_in, g, j, 0, 16)
                done(v, s_turn, g, j, SLOTS)
                done(v, s_hot_f, g, j, SLOTS)
                for k in range(TILES):
                    ins = nc.vector.tensor_scalar(hot[:, j, k, :], t["node_no"][:, bass.ds(win * P, P)],
                                                  ends[:, j, k, 1:2], None, ALU.is_equal)
                ins.then_inc(s_hot[j], 1)

            def sums(g, j):
                done(v, s_prod, g, j, 0)
                done(v, src_in, g, j, 0, 32)
                done(v, s_soft, g, j, SLOTS)
                nc.vector.tensor_tensor(pre[:, j], pre_ps[:, j % 2], from_src[:, j], ALU.add).then_inc(s_pre[j], 1)

            def magnitude(g, j):
                done(v, s_pre, g, j, 0)
                done(v, s_expo, g, j, 2)
                nc.vector.scalar_tensor_tensor(size[:, j % 2], pre[:, j, :, F:F2], -1.0, pre[:, j, :, F:F2],
                                               ALU.mult, ALU.max).then_inc(s_abs[j], 1)

            def softplus(g, j):
                done(v, s_logs, g, j, 0)
                nc.vector.scalar_tensor_tensor(logs[:, j, :, F:F2], pre[:, j, :, F:F2], 0.0, logs[:, j, :, F:F2],
                                               ALU.max, ALU.add).then_inc(s_soft[j], 1)

            def message(g, j):
                done(v, s_soft, g, j, 0)
                done(v, s_gate, g, j, 0)
                done(v, s_sum, g, j, 2)
                nc.vector.tensor_tensor(msg[:, j % 2, :, 0:F], logs[:, j, :, F:F2], logs[:, j, :, 0:F], ALU.mult
                                        ).then_inc(s_msg[j], 1)

            def add_up(g, j, win):
                done(v, s_sum, g, j, 0)
                done(v, s_added, g, j, 1)
                rows = t["sums"][:, bass.ds(win * (F + 1), F + 1)]
                nc.vector.tensor_tensor(rows, sum_ps[:, j % 2, 0:F + 1], rows, ALU.add).then_inc(s_added[j], 1)

            LAST = 5

            def stages(g, j, hot_win, sum_win, live=lambda lag, j: True):
                if live(0, j):
                    one_hot(g, j, hot_win)
                if live(2, j) and (b := back(g, j, 2)):
                    sums(*b)
                if live(4, j) and (b := back(g, j, 4)):
                    softplus(*b)
                if live(2, j) and (b := back(g, j, 2)):
                    magnitude(*b)
                if live(4, j) and (b := back(g, j, 4)):
                    message(*b)
                if live(LAST, j) and (b := back(g, j, LAST)):
                    add_up(*b, sum_win)

            def one(g):
                v.wait_ge(win_tab, g * 16 + 16)
                v.sem_inc(passed, 1)
                first = BEFORE - LAST
                w = load_windows(v, mybir.EngineType.DVE, first, BEFORE + SLOTS - first)
                v.sem_inc(dve_has, 1)
                for j in range(SLOTS):
                    stages(g, j, w[LAST + j], w[j])

            def drain(g):
                w = load_windows(v, mybir.EngineType.DVE, BEFORE + SLOTS - LAST, LAST)
                for step in range(LAST):
                    stages(g + step // SLOTS, step % SLOTS, None, w[step], lambda lag, _: step < lag)
                v.wait_ge(s_added[SLOTS - 1], g)
                v.sem_inc(passed, 1)
            turns(v, groups, one, drain, peeled=2)


def set_up(nc, t, d):
    with nc.cleanup_on_exit(), ExitStack() as ctx:
        sem = lambda name: nc.alloc_semaphore(name)
        vec = ctx.enter_context(nc.sbuf_tensor("bn_vec", [P, 2, 4, F], F32))
        root = ctx.enter_context(nc.sbuf_tensor("bn_root", [P, 2, F], F32))
        inv = ctx.enter_context(nc.sbuf_tensor("bn_inv", [P, 2, F], F32))
        loaded, nodes_in, filled, rooted, chain = (sem(n) for n in (
            "bn_in", "nodes_in", "filled", "rooted", "bn_chain"))
        block = ctx.enter_context(nc.Block())

        @block.sync
        def _(sp):
            for layer in (1, 2):
                for k, name in enumerate(("gamma", "beta", "rmean", "rvar")):
                    sp.dma_start(vec[:, layer - 1, k, :], d[f"W{layer}"][name].rearrange("(a f) -> a f", a=1)
                                 .to_broadcast([P, F])).then_inc(loaded, 16)
            sp.dma_start(t["x_nodes"][:].rearrange("p (w f) -> p w f", f=F),
                         d["x"].rearrange("(w p) f -> p w f", p=P)).then_inc(nodes_in, 16)

        @block.gpsimd
        def _(pool):
            for name in ("ident", "ident_b"):
                nc.gpsimd.memset(t[name][:], 0.0).then_inc(filled, 1)
            for n, name in enumerate(("ident", "ident_b")):
                pool.wait_ge(filled, 2 + n)
                nc.gpsimd.affine_select(out=t[name][:], in_=t[name][:], compare_op=ALU.not_equal, fill=1.0, base=0,
                                        pattern=[[-1, P]], channel_multiplier=1).then_inc(filled, 1)
            pool.wait_ge(filled, 4)

        @block.scalar
        def _(act):
            act.wait_ge(chain, 1)
            nc.scalar.activation(root[:], vec[:, :, 3, :], ACT.Sqrt).then_inc(rooted, 1)

        @block.vector
        def _(v):
            n = [0]

            def after(ins):
                n[0] += 1
                ins.then_inc(chain, 1)
                v.wait_ge(chain, n[0])

            v.wait_ge(loaded, 16 * 8)
            after(nc.vector.tensor_scalar(vec[:, :, 3, :], vec[:, :, 3, :], BN_EPS, None, ALU.add))
            v.wait_ge(rooted, 1)
            after(nc.vector.reciprocal(inv[:], root[:]))
            v.wait_ge(nodes_in, 16)
            for k in range(2):
                scale, shift = t[f"bn_scale{k + 1}"], t[f"bn_shift{k + 1}"]
                after(nc.vector.tensor_tensor(scale[:], inv[:, k, :], vec[:, k, 0, :], ALU.mult))
                after(nc.vector.tensor_tensor(shift[:], vec[:, k, 2, :], scale[:], ALU.mult))
                after(nc.vector.tensor_tensor(shift[:], vec[:, k, 1, :], shift[:], ALU.subtract))
            nodes = t["x_nodes"][:].rearrange("p (w f) -> p w f", f=F)
            after(nc.vector.tensor_tensor(nodes, nodes, t["bn_shift1"][:].unsqueeze(1).to_broadcast([P, WPAD, F]),
                                          ALU.add))


def inverse_counts(nc, t, layer):
    with nc.cleanup_on_exit(), ExitStack() as ctx:
        s = nc.alloc_semaphore(f"count_chain{layer}")
        block = ctx.enter_context(nc.Block())

        @block.vector
        def _(v):
            counts = t["sums"][:].rearrange("p (w f) -> p w f", f=F + 1)[:, :, F]
            nc.vector.tensor_scalar(t["per_count"][:, 0:WPAD], counts, 1.0, None, ALU.max).then_inc(s, 1)
            v.wait_ge(s, 1)
            nc.vector.reciprocal(t["per_count"][:, 0:WPAD], t["per_count"][:, 0:WPAD]).then_inc(s, 1)
            v.wait_ge(s, 2)


def finish(nc, t, d, out):
    with nc.cleanup_on_exit(), ExitStack() as ctx:
        sem = lambda name: nc.alloc_semaphore(name)
        sb = lambda name, shape: ctx.enter_context(nc.sbuf_tensor(name, shape, F32))
        mean, var, eps = sb("mean", [P, WINDOWS]), sb("var", [P, WINDOWS]), sb("ln_eps", [P, 1])
        x_again, chain, squared, rooted, stored = (sem(n) for n in (
            "x_again", "ln_chain", "squared", "ln_rooted", "stored"))
        wide = lambda a: a.unsqueeze(2).to_broadcast([P, WINDOWS, F])
        x0 = t["node_no"][:].rearrange("p (w f) -> p w f", f=F)
        y = t["x_nodes"][:].rearrange("p (w f) -> p w f", f=F)[:, 0:WINDOWS, :]
        sums = t["sums"][:].rearrange("p (w f) -> p w f", f=F + 1)[:, 0:WINDOWS, 0:F]
        whole = NODES // P
        left = NODES - whole * P
        block = ctx.enter_context(nc.Block())

        @block.sync
        def _(sp):
            sp.dma_start(x0, d["x"][0:WINDOWS * P, :].rearrange("(w p) f -> p w f", p=P)).then_inc(x_again, 16)
            sp.wait_ge(chain, 12)
            sp.dma_start(out[0:whole * P, :].rearrange("(w p) f -> p w f", p=P), y[:, 0:whole, :]).then_inc(stored, 16)
            sp.dma_start(out[whole * P:NODES, :], y[0:left, whole, :]).then_inc(stored, 16)
            sp.wait_ge(stored, 32)

        @block.scalar
        def _(act):
            act.wait_ge(chain, 8)
            nc.scalar.activation(sums, y, ACT.Square).then_inc(squared, 1)
            act.wait_ge(chain, 10)
            nc.scalar.activation(var[:], var[:], ACT.Sqrt).then_inc(rooted, 1)

        @block.vector
        def _(v):
            n = [0]

            def after(ins):
                n[0] += 1
                ins.then_inc(chain, 1)
                v.wait_ge(chain, n[0])

            tt = nc.vector.tensor_tensor
            after(tt(sums, sums, wide(t["per_count"][:, 0:WINDOWS]), ALU.mult))
            after(tt(sums, sums, t["bn_scale2"][:].unsqueeze(1).to_broadcast([P, WINDOWS, F]), ALU.mult))
            after(tt(y, y, sums, ALU.add))
            after(tt(y, y, t["bn_shift2"][:].unsqueeze(1).to_broadcast([P, WINDOWS, F]), ALU.add))
            v.wait_ge(x_again, 16)
            after(tt(y, y, x0, ALU.add))
            after(nc.vector.tensor_reduce(mean[:], y, AX.X, ALU.add))
            after(nc.vector.tensor_scalar(mean[:], mean[:], 1.0 / F, None, ALU.mult))
            after(tt(y, y, wide(mean[:]), ALU.subtract))
            v.wait_ge(squared, 1)
            after(nc.vector.tensor_reduce(var[:], sums, AX.X, ALU.add))
            after(nc.vector.tensor_scalar(var[:], var[:], 1.0 / F, LN_EPS, ALU.mult, ALU.add))
            v.wait_ge(rooted, 1)
            after(nc.vector.reciprocal(var[:], var[:]))
            after(tt(y, y, wide(var[:]), ALU.mult))


def graph_layers(nc, d, out):
    with ExitStack() as ctx:
        sb = lambda name, shape, dt: ctx.enter_context(nc.sbuf_tensor(name, shape, dt))
        ctx.enter_context(nc.allow_non_contiguous_dma(reason="16-byte rows of edge ends, and small tables"))
        t = {
            "off_dram": nc.dram_tensor("off_table", [TABLE], I32, kind="Internal").ap(),
            "win_dram": nc.dram_tensor("win_table", [TABLE], I32, kind="Internal").ap(),
            "src_dram1": nc.dram_tensor("src_rows1", [NPAD, F2], F32, kind="Internal").ap(),
            "src_dram2": nc.dram_tensor("src_rows2", [NPAD, F2], F32, kind="Internal").ap(),
            "choice": sb("choice", [1, 2], I32),
            "node_no": sb("node_no", [P, WINDOWS * P], F32),
            "sums": sb("sums", [P, WPAD * (F + 1)], F32),
            "per_count": sb("per_count", [P, WPAD], F32),
            "ident": sb("ident", [P, P], F32),
            "ident_b": sb("ident_b", [P, P], BF16),
            "bn_scale1": sb("bn_scale1", [P, F], F32), "bn_shift1": sb("bn_shift1", [P, F], F32),
            "bn_scale2": sb("bn_scale2", [P, F], F32), "bn_shift2": sb("bn_shift2", [P, F], F32),
        }
        plan_steps(nc, t, d)
        t["x_nodes"] = sb("x_nodes", [P, WPAD * F], F32)
        t["dst_parts"] = sb("dst_parts", [P, WPAD * 3 * F2], BF16)
        set_up(nc, t, d)
        layer_tables(nc, t, d, 1)
        edge_loop(nc, t, d, 1)
        inverse_counts(nc, t, 1)
        layer_tables(nc, t, d, 2)
        edge_loop(nc, t, d, 2)
        finish(nc, t, d, out)


def kernel(**inputs):
    import concourse.bacc as bacc
    from concourse.bass_utils import run_bass_kernel_spmd

    a = {k: np.asarray(v) for k, v in inputs.items()}
    nc = bacc.Bacc("TRN2", target_bir_lowering=False, num_devices=1)
    arrays = {}

    def given(name, array):
        array = np.ascontiguousarray(array)
        arrays[name] = array
        return nc.dram_tensor(name, array.shape, mybir.dt.from_np(array.dtype), kind="ExternalInput").ap()

    x = np.zeros((NPAD, F), a["x"].dtype)
    x[:NODES] = a["x"]
    ends = np.zeros((EPAD, 2), a["src"].dtype)
    ends[:, 1] = NO_WINDOW
    ends[:EDGES, 0] = a["src"]
    ends[:EDGES, 1] = a["dst"]
    dst = np.full((EPAD + P,), NO_WINDOW, a["dst"].dtype)
    dst[:EDGES] = a["dst"]
    edge_t = np.zeros((FE, EPAD), a["edge_attr_64"].dtype)
    edge_t[:, :EDGES] = a["edge_attr_64"].T
    d = {
        "x": given("x_rows", x), "xT": given("x_cols", x.T), "ends": given("edge_ends", ends),
        "dst": given("destinations", dst), "edge_t": given("edge_cols", edge_t),
    }
    for layer in (1, 2):
        p = {k: a[f"L0_gnn_{k}{layer}"] for k in ("Wf", "bf", "Ws", "bs", "gamma", "beta", "rmean", "rvar")}
        both = np.concatenate([p["Wf"], p["Ws"]], axis=1)
        d[f"W{layer}"] = {
            "node": given(f"in_w_node{layer}", np.concatenate([both[:F], both[F:2 * F]], axis=1)),
            "edge": given(f"in_w_edge{layer}", both[2 * F:]),
            "bias": given(f"in_bias{layer}", np.concatenate([p["bf"], p["bs"]])),
            **{k: given(f"{k}{layer}", p[k]) for k in ("gamma", "beta", "rmean", "rvar")},
        }
    out = nc.dram_tensor("out", (NODES, F), F32, kind="ExternalOutput").ap()
    graph_layers(nc, d, out)
    r = run_bass_kernel_spmd(nc, [arrays], core_ids=[0])
    return r.results[0]["out"]
```

```python
from contextlib import ExitStack

import numpy as np

import concourse.bass as bass
from concourse import mybir

ALU = mybir.AluOpType
ACT = mybir.ActivationFunctionType
AX = mybir.AxisListType
F32 = mybir.dt.float32
BF16 = mybir.dt.bfloat16
I32 = mybir.dt.int32
U32 = mybir.dt.uint32

P = 128
NODES = 6250
EDGES = 100000
F = 128
FE = 64
F2 = 2 * F
BN_EPS = 1e-5
LN_EPS = 1e-5

WINDOWS = -(-NODES // P)
TURN = 4
WPAD = -(-WINDOWS // TURN) * TURN
NPAD = WPAD * P
TILES = 2
STEP = TILES * P
SOFT_MAX = 20.0
SLOTS = 4
BODY = 5
EPAD = -(-(EDGES + STEP) // P) * P
NO_WINDOW = NPAD + 1024
ECOLS = EPAD // P
SORTED_GROUPS = -(-((EDGES + WINDOWS * (STEP - 1)) // STEP) // (BODY * SLOTS)) * BODY
SORTED_STEPS = SORTED_GROUPS * SLOTS
SCOLS = -(-SORTED_STEPS // P)
BLOCKS = -(-EDGES // STEP)
GENERAL_GROUPS = -(-(BLOCKS * WINDOWS) // (BODY * SLOTS)) * BODY
GENERAL_STEPS = GENERAL_GROUPS * SLOTS
BEFORE = 2 * SLOTS
SORTED_AT = BEFORE
GENERAL_AT = SORTED_AT + SCOLS * P + BEFORE
TABLE = GENERAL_AT + GENERAL_STEPS + SLOTS


def plan_steps(nc, t, d):
    with nc.cleanup_on_exit(), ExitStack() as ctx:
        sb = lambda name, shape, dt: ctx.enter_context(nc.sbuf_tensor(name, shape, dt))
        sem = lambda name: nc.alloc_semaphore(name)
        dst_i = sb("dst_i", [P, 2, ECOLS], I32)
        dst_f = sb("dst_f", [P, 2, ECOLS], F32)
        below = sb("below", [P, ECOLS], F32)
        counts = sb("counts", [P, WINDOWS + 1], F32)
        ones = sb("ones", [P, P], F32)
        total = sb("total", [P, WINDOWS + 1], F32)
        in_window = sb("in_window", [P, WINDOWS], F32)
        steps_i = sb("steps_i", [P, WINDOWS], I32)
        steps_f = sb("steps_f", [P, WINDOWS], F32)
        step_end = sb("step_end", [P, WINDOWS], F32)
        shift = sb("shift", [P, WINDOWS], F32)
        step_no = sb("step_no", [P, SCOLS], F32)
        passed = sb("passed", [P, SCOLS, WINDOWS], F32)
        shifted = sb("shifted", [P, SCOLS, WINDOWS], F32)
        win_f = sb("win_f", [P, SCOLS], F32)
        off_f = sb("off_f", [P, SCOLS], F32)
        entry = sb("entry", [P, 2, SCOLS], I32)
        flag_f = sb("flag_f", [1, 4], F32)
        gen_off = sb("gen_off", [WINDOWS, BLOCKS], I32)
        gen_win = sb("gen_win", [WINDOWS, BLOCKS], I32)
        tail = sb("tail", [1, 2, (BODY + 1) * SLOTS], I32)
        edges_below = sb("edges_below", [P, WINDOWS], F32)
        signs = sb("signs", [P, ECOLS], F32)
        total_ps = ctx.enter_context(nc.psum_tensor("total_ps", [P, 512], F32))
        vec = sb("bn_vec", [P, 2, 4, F], F32)
        root = sb("bn_root", [P, 2, F], F32)
        inv = sb("bn_inv", [P, 2, F], F32)
        BY_DVE = WINDOWS // 2

        dst_in = sem("dst_in")
        iotas = sem("iotas")
        dve = sem("dve_done")
        summed = sem("summed")
        written = sem("written")
        converted = sem("converted")
        signs_done = sem("signs_done")
        bn_in, nodes_in, filled, rooted, eps_added = (sem(n) for n in (
            "bn_in", "nodes_in", "filled", "rooted", "eps_added"))
        general = t["off_dram"][GENERAL_AT:GENERAL_AT + WINDOWS * BLOCKS].rearrange("(w k) -> w k", k=BLOCKS)
        general_w = t["win_dram"][GENERAL_AT:GENERAL_AT + WINDOWS * BLOCKS].rearrange("(w k) -> w k", k=BLOCKS)
        rest = TABLE - GENERAL_AT - WINDOWS * BLOCKS
        sorted_off = t["off_dram"][SORTED_AT:SORTED_AT + SCOLS * P].rearrange("(p c) -> p c", c=SCOLS)
        sorted_win = t["win_dram"][SORTED_AT:SORTED_AT + SCOLS * P].rearrange("(p c) -> p c", c=SCOLS)

        block = ctx.enter_context(nc.Block())

        @block.sync
        def _(sp):
            sp.dma_start(dst_i[:, 0, :], d["dst"][0:EPAD].rearrange("(p c) -> p c", c=ECOLS)).then_inc(dst_in, 16)
            sp.dma_start(dst_i[:, 1, :], d["dst"][1:EPAD + 1].rearrange("(p c) -> p c", c=ECOLS)).then_inc(dst_in, 16)
            for layer in (1, 2):
                for k, name in enumerate(("gamma", "beta", "rmean", "rvar")):
                    sp.dma_start(vec[:, layer - 1, k, :], d[f"W{layer}"][name].rearrange("(a f) -> a f", a=1)
                                 .to_broadcast([P, F])).then_inc(bn_in, 16)
            sp.dma_start(t["x_nodes"][:].rearrange("p (w f) -> p w f", f=F),
                         d["x"].rearrange("(w p) f -> p w f", p=P)).then_inc(nodes_in, 16)
            sp.wait_ge(iotas, 6)
            sp.dma_start(general, gen_off[:]).then_inc(written, 16)
            sp.dma_start(general_w, gen_win[:]).then_inc(written, 16)
            n = 2
            for table, k in ((t["off_dram"], 0), (t["win_dram"], 1)):
                for at, many in ((0, BEFORE), (GENERAL_AT - BEFORE, BEFORE), (TABLE - rest, rest)):
                    if many:
                        sp.dma_start(table[at:at + many].rearrange("(a c) -> a c", a=1),
                                     tail[:, k, 0:many]).then_inc(written, 16)
                        n += 1
            sp.wait_ge(dve, 1)
            sp.dma_start(sorted_off, entry[:, 0, :]).then_inc(written, 16)
            sp.dma_start(sorted_win, entry[:, 1, :]).then_inc(written, 16)
            sp.wait_ge(written, 16 * (n + 2))

        @block.gpsimd
        def _(pool):
            nc.gpsimd.iota(edges_below[:], [[-2 * P, WINDOWS]], base=1 - 2 * P, channel_multiplier=0,
                           allow_small_or_imprecise_dtypes=True).then_inc(iotas, 1)
            nc.gpsimd.iota(step_no[:], [[1, SCOLS]], base=0, channel_multiplier=SCOLS,
                           allow_small_or_imprecise_dtypes=True).then_inc(iotas, 1)
            nc.gpsimd.iota(gen_off[:], [[STEP, BLOCKS]], base=0, channel_multiplier=0).then_inc(iotas, 1)
            nc.gpsimd.iota(gen_win[:], [[0, BLOCKS]], base=0, channel_multiplier=1).then_inc(iotas, 1)
            nc.gpsimd.iota(tail[:, 0, :], [[0, (BODY + 1) * SLOTS]], base=EDGES, channel_multiplier=0).then_inc(iotas, 1)
            nc.gpsimd.iota(tail[:, 1, :], [[0, (BODY + 1) * SLOTS]], base=WINDOWS - 1, channel_multiplier=0).then_inc(iotas, 1)
            nc.gpsimd.iota(t["node_no"][:], [[1, WINDOWS * P]], base=0, channel_multiplier=0,
                           allow_small_or_imprecise_dtypes=True).then_inc(iotas, 1)
            for name in ("ident", "ident_b"):
                nc.gpsimd.memset(t[name][:], 0.0).then_inc(filled, 1)
            for n, name in enumerate(("ident", "ident_b")):
                pool.wait_ge(filled, 2 + n)
                nc.gpsimd.affine_select(out=t[name][:], in_=t[name][:], compare_op=ALU.not_equal, fill=1.0, base=0,
                                        pattern=[[-1, P]], channel_multiplier=1).then_inc(filled, 1)
            pool.wait_ge(filled, 4)

        @block.scalar
        def _(act):
            act.wait_ge(converted, 1)
            act.wait_ge(iotas, 1)
            for n, w in enumerate(range(BY_DVE, WINDOWS)):
                if n:
                    act.wait_ge(signs_done, n)
                nc.scalar.activation(signs[:], dst_f[:, 0, :], ACT.Sign, bias=edges_below[:, w:w + 1], scale=2.0,
                                     accum_out=counts[:, w:w + 1]).then_inc(signs_done, 1)
            act.wait_ge(eps_added, 1)
            nc.scalar.activation(root[:], vec[:, :, 3, :], ACT.Sqrt).then_inc(rooted, 1)

        @block.tensor
        def _(pe):
            pe.wait_ge(summed, 1)
            nc.tensor.matmul(total_ps[:, 0:WINDOWS + 1], ones[:], counts[:], start=True, stop=True).then_inc(summed, 1)

        @block.vector
        def _(v):
            own = sem("plan_chain")
            n = [0]

            def after(ins):
                n[0] += 1
                ins.then_inc(own, 1)
                v.wait_ge(own, n[0])

            nc.vector.memset(ones[:], 1.0)
            v.wait_ge(dst_in, 32)
            after(nc.vector.tensor_copy(dst_f[:], dst_i[:]))
            v.sem_inc(converted, 1)
            after(nc.vector.tensor_tensor(below[:], dst_f[:, 0, :], dst_f[:, 1, :], ALU.is_gt))
            after(nc.vector.tensor_reduce(counts[:, WINDOWS:WINDOWS + 1], below[:], AX.X, ALU.add))
            for w in range(BY_DVE):
                last = nc.vector.tensor_scalar(below[:], dst_f[:, 0, :], float(P * (w + 1)), None, ALU.is_lt,
                                               ALU.add, accum_out=counts[:, w:w + 1])
                after(last)
            v.wait_ge(signs_done, WINDOWS - BY_DVE)
            after(nc.vector.tensor_scalar(counts[:, BY_DVE:WINDOWS], counts[:, BY_DVE:WINDOWS], -0.5, ECOLS / 2.0,
                                          ALU.mult, ALU.add))
            v.sem_inc(summed, 1)
            v.wait_ge(bn_in, 16 * 8)
            nc.vector.tensor_scalar(vec[:, :, 3, :], vec[:, :, 3, :], BN_EPS, None, ALU.add).then_inc(eps_added, 1)
            v.wait_ge(summed, 2)
            after(nc.vector.tensor_copy(total[:], total_ps[:, 0:WINDOWS + 1]))
            nc.vector.tensor_copy(in_window[:, 0:1], total[:, 0:1])
            after(nc.vector.tensor_tensor(in_window[:, 1:], total[:, 1:WINDOWS], total[:, 0:WINDOWS - 1], ALU.subtract))
            after(nc.vector.tensor_scalar(steps_i[:], in_window[:], float(STEP - 1), None, ALU.add))
            after(nc.vector.tensor_scalar(steps_i[:], steps_i[:], STEP.bit_length() - 1, None, ALU.arith_shift_right))
            after(nc.vector.tensor_copy(steps_f[:], steps_i[:]))
            after(nc.vector.tensor_tensor_scan(step_end[:], steps_f[:], steps_f[:], 0.0, ALU.add, ALU.bypass))
            after(nc.vector.scalar_tensor_tensor(shift[:], steps_f[:], -float(STEP), in_window[:], ALU.mult, ALU.add))
            v.wait_ge(iotas, 7)
            for c in range(SCOLS):
                after(nc.vector.tensor_scalar(passed[:, c, :], step_end[:], step_no[:, c:c + 1], None, ALU.is_le))
                after(nc.vector.tensor_tensor(shifted[:, c, :], passed[:, c, :], shift[:], ALU.mult))
            after(nc.vector.tensor_reduce(win_f[:], passed[:], AX.X, ALU.add))
            after(nc.vector.tensor_reduce(off_f[:], shifted[:], AX.X, ALU.add))
            after(nc.vector.scalar_tensor_tensor(off_f[:], step_no[:], float(STEP), off_f[:], ALU.mult, ALU.add))
            after(nc.vector.tensor_scalar(entry[:, 0, :], off_f[:], float(EDGES), None, ALU.min))
            after(nc.vector.tensor_scalar(flag_f[:, 0:1], total[0:1, WINDOWS:WINDOWS + 1], 1.0, None, ALU.min))
            after(nc.vector.tensor_scalar(t["choice"][:, 0:1], flag_f[:, 0:1],
                                          float((GENERAL_GROUPS - SORTED_GROUPS) // BODY),
                                          float(SORTED_GROUPS // BODY - 1), ALU.mult, ALU.add))
            after(nc.vector.tensor_scalar(t["choice"][:, 1:2], flag_f[:, 0:1], float(GENERAL_AT - SORTED_AT),
                                          None, ALU.mult))
            nc.vector.tensor_scalar(entry[:, 1, :], win_f[:], float(WINDOWS - 1), None, ALU.min).then_inc(dve, 1)
            v.wait_ge(rooted, 1)
            after(nc.vector.reciprocal(inv[:], root[:]))
            for k in range(2):
                scale, shift_k = t[f"bn_scale{k + 1}"], t[f"bn_shift{k + 1}"]
                after(nc.vector.tensor_tensor(scale[:], inv[:, k, :], vec[:, k, 0, :], ALU.mult))
                after(nc.vector.tensor_tensor(shift_k[:], vec[:, k, 2, :], scale[:], ALU.mult))
                after(nc.vector.tensor_tensor(shift_k[:], vec[:, k, 1, :], shift_k[:], ALU.subtract))
            v.wait_ge(nodes_in, 16)
            nodes = t["x_nodes"][:].rearrange("p (w f) -> p w f", f=F)
            after(nc.vector.tensor_tensor(nodes, nodes, t["bn_shift1"][:].unsqueeze(1).to_broadcast([P, WPAD, F]),
                                          ALU.add))
            v.wait_ge(dve, 1)


def layer_tables(nc, t, d, layer):
    with nc.cleanup_on_exit(), ExitStack() as ctx:
        sb = lambda name, shape, dt: ctx.enter_context(nc.sbuf_tensor(f"{name}{layer}", shape, dt))
        sem = lambda name: nc.alloc_semaphore(f"{name}{layer}")
        ps = lambda name, shape, dt: ctx.enter_context(nc.psum_tensor(f"{name}{layer}", shape, dt))
        second = layer == 2
        w_node = sb("w_node", [P, 2 * F2], F32)
        bias = sb("bias", [P, F2], F32)
        x_t = sb("x_t", [P, TURN, P], F32)
        dst_part = sb("dst_part", [P, TURN, F2], F32)
        rest = sb("rest", [P, TURN, F2], F32)
        src_part = sb("src_part", [P, TURN, F2], F32)
        scaled = sb("scaled", [P, 2, F], F32)
        x_new = sb("x_new", [P, 2, F], F32)
        dst_ps = ps("dst_ps", [P, 2, 512], F32)
        src_ps = ps("src_ps", [P, 2, 512], F32)
        turned = ps("turned", [P, 2, 512], F32)

        loaded = sem("weights_in")
        x_in = [sem(f"x_in{s}") for s in range(TURN)]
        x_ready = sem("x_ready")
        x_turned = sem("x_turned")
        x_scaled = sem("x_scaled")
        x_kept = sem("x_kept")
        prod_done = sem("prod_done")
        dst_done = sem("dst_done")
        part1 = sem("part1")
        rest1 = sem("rest1")
        part2 = sem("part2")
        part3 = sem("part3")
        src_done = sem("src_done")
        src_out = [sem(f"src_out{s}") for s in range(TURN)]
        W, parts, win3 = d[f"W{layer}"], t["dst_parts"], 3 * F2

        own = sem("scaled")
        negated = sem("node_weights_negated")
        LAST, PEELED = 7, 2

        block = ctx.enter_context(nc.Block())

        def windows(eng, one, lag):
            for u in range(TURN * PEELED):
                one(u, u % TURN, lambda k: u >= k)
            with eng.Fori(PEELED, WPAD // TURN) as q:
                for s in range(TURN):
                    one(q * TURN + s, s, lambda k: True)
            for u in range(WPAD, WPAD + lag):
                one(u, u % TURN, lambda k: u - k < WPAD)

        def nth(eng, signal, w, back=0):
            if isinstance(w, int) and w < back:
                return
            eng.wait_ge(signal, w + (1 - back))

        def in_slot(eng, signals, w, s, back=0):
            if isinstance(w, int):
                if w >= back:
                    eng.wait_ge(signals[s], 16 * ((w - back) // TURN + 1))
            else:
                eng.wait_ge(signals[s], w * (16 // TURN) + (16 - 16 // TURN * (back + s)))

        @block.sync
        def _(sp):
            sp.dma_start(w_node[:], W["node"]).then_inc(loaded, 16)
            sp.dma_start(bias[:], W["bias"].rearrange("(a f) -> a f", a=1).to_broadcast([P, F2])).then_inc(loaded, 16)

            def load_x(w, s, within):
                nth(sp, prod_done, w, back=TURN)
                sp.dma_start(x_t[:, s, :], d["xT"][:, bass.ds(w * P, P)]).then_inc(x_in[s], 16)
            if not second:
                windows(sp, load_x, 0)

        @block.gpsimd
        def _(pool):
            def store(w, s, within):
                nth(pool, src_done, w)
                pool.dma_start(t[f"src_dram{layer}"][bass.ds(w * P, P), :], src_part[:, s, :]).then_inc(src_out[s], 16)
            windows(pool, store, 0)
            for s in range(TURN):
                pool.wait_ge(src_out[s], 16 * (WPAD // TURN))

        @block.tensor
        def _(pe):
            pe.wait_ge(negated, 2)

            def transpose(w, s):
                nth(pe, x_scaled, w)
                nc.tensor.transpose(turned[:, s % 2, 0:P], x_new[:, s % 2, :], t["ident"][:]).then_inc(x_turned, 1)

            def product(w, s):
                if second:
                    nth(pe, x_ready, w)
                else:
                    in_slot(pe, x_in, w, s)
                nth(pe, dst_done, w, back=2)
                nth(pe, src_done, w, back=2)
                nc.tensor.matmul(dst_ps[:, s % 2, 0:F2], x_t[:, s, :], w_node[:, 0:F2], start=True, stop=True)
                nc.tensor.matmul(src_ps[:, s % 2, 0:F2], x_t[:, s, :], w_node[:, F2:2 * F2], start=True, stop=True
                                 ).then_inc(prod_done, 1)

            def one(u, s, within):
                if second and within(0):
                    transpose(u, s)
                if within(1):
                    product(u + (-1), (s - 1) % TURN)
            windows(pe, one, 1)

        @block.scalar
        def _(act):
            def keep_x(w, s):
                nth(act, x_turned, w)
                nth(act, prod_done, w, back=TURN)
                nc.scalar.copy(x_t[:, s, :], turned[:, s % 2, 0:P]).then_inc(x_ready, 1)
                nc.scalar.copy(t["x_nodes"][:, bass.ds(w * F, F)], x_new[:, s % 2, :]).then_inc(x_kept, 1)

            def copy_source(w, s):
                nth(act, prod_done, w)
                in_slot(act, src_out, w, s, back=TURN)
                nc.scalar.copy(src_part[:, s, :], src_ps[:, s % 2, 0:F2]).then_inc(src_done, 1)

            def make_part1(w, s):
                nth(act, dst_done, w)
                nc.scalar.copy(parts[:, bass.ds(w * win3, F2)], dst_part[:, s, :]).then_inc(part1, 1)

            def make_part2(w, s):
                nth(act, rest1, w)
                nc.scalar.copy(parts[:, bass.ds(w * win3 + F2, F2)], rest[:, s, :]).then_inc(part2, 1)

            def one(u, s, within):
                if second and within(0):
                    keep_x(u, s)
                if within(2):
                    copy_source(u + (-2), (s - 2) % TURN)
                    make_part1(u + (-2), (s - 2) % TURN)
                if within(4):
                    make_part2(u + (-4), (s - 4) % TURN)
            windows(act, one, 4)

        @block.vector
        def _(v):
            v.wait_ge(loaded, 32)
            gates = w_node[:].rearrange("p (h f) -> p h f", f=F)[:, 0:4:2, :]
            nc.vector.tensor_scalar(gates, gates, -1.0, None, ALU.mult).then_inc(negated, 1)
            nc.vector.tensor_scalar(bias[:, 0:F], bias[:, 0:F], -1.0, None, ALU.mult).then_inc(negated, 1)
            v.wait_ge(negated, 2)

            def scale(w, s):
                nth(v, x_scaled, w, back=2)
                nc.vector.scalar_tensor_tensor(
                    scaled[:, s % 2, :], t["sums"][:, bass.ds(w * (F + 1), F)], t["per_count"][:, bass.ds(w, 1)],
                    t["bn_scale1"][:], ALU.mult, ALU.mult).then_inc(own, 1)

            def make_x(w, s):
                nth(v, own, w)
                nth(v, x_kept, w, back=2)
                nc.vector.tensor_tensor(x_new[:, s % 2, :], t["x_nodes"][:, bass.ds(w * F, F)], scaled[:, s % 2, :],
                                        ALU.add).then_inc(x_scaled, 1)

            def add_bias(w, s):
                nth(v, prod_done, w)
                nth(v, rest1, w, back=TURN)
                nc.vector.tensor_tensor(dst_part[:, s, :], dst_ps[:, s % 2, 0:F2], bias[:], ALU.add).then_inc(dst_done, 1)

            def make_rest(w, s):
                nth(v, part1, w)
                nth(v, part3, w, back=TURN)
                nc.vector.tensor_tensor(rest[:, s, :], dst_part[:, s, :], parts[:, bass.ds(w * win3, F2)],
                                        ALU.subtract).then_inc(rest1, 1)

            def make_part3(w, s):
                nth(v, part2, w)
                nc.vector.tensor_tensor(parts[:, bass.ds(w * win3 + 2 * F2, F2)], rest[:, s, :],
                                        parts[:, bass.ds(w * win3 + F2, F2)], ALU.subtract).then_inc(part3, 1)

            def one(u, s, within):
                if second and within(1):
                    make_x(u + (-1), (s - 1) % TURN)
                if second and within(0):
                    scale(u, s)
                if within(7):
                    make_part3(u + (-7), (s - 7) % TURN)
                if within(5):
                    make_rest(u + (-5), (s - 5) % TURN)
                if within(3):
                    add_bias(u + (-3), (s - 3) % TURN)
            windows(v, one, LAST)


def edge_loop(nc, t, d, layer):
    with nc.cleanup_on_exit(), ExitStack() as ctx:
        sb = lambda name, shape, dt: ctx.enter_context(nc.sbuf_tensor(f"{name}{layer}", shape, dt))
        ps = lambda name, shape, dt: ctx.enter_context(nc.psum_tensor(f"{name}{layer}", shape, dt))
        sem = lambda name: nc.alloc_semaphore(f"{name}{layer}")
        each = lambda name: [nc.alloc_semaphore(f"{name}{layer}_{j}") for j in range(SLOTS)]

        w_edge = sb("w_edge", [FE, F2], F32)
        sp_off = sb("sp_off", [1, SLOTS + 1], I32)
        wins = sb("wins", [1, BEFORE + SLOTS], I32)
        ends = sb("ends", [P, SLOTS, TILES, 2], I32)
        edge_t = sb("edge_t", [FE, SLOTS, STEP], F32)
        from_src = sb("from_src", [P, SLOTS, TILES, F2], F32)
        hot = sb("hot", [P, SLOTS, TILES, P], BF16)
        hot_t = sb("hot_t", [P, SLOTS, TILES, P], BF16)
        hot_f = sb("hot_f", [P, SLOTS, TILES, P], F32)
        pre = sb("pre", [P, SLOTS, TILES, 3 * F], F32)
        logs = sb("logs", [P, SLOTS, TILES, F2], F32)
        msg = sb("msg", [P, 2, TILES, F + 1], F32)
        turn_ps = ps("turn_ps", [P, 2, 1024], BF16)
        pre_ps = ps("pre_ps", [P, 2, TILES, F2], F32)
        sum_ps = ps("sum_ps", [P, 2, 512], F32)

        w_in = sem("w_edge_in")
        sp_tab = sem("sp_table_in")
        win_tab = sem("windows_in")
        pe_has = sem("pe_has_windows")
        dve_has = sem("dve_has_windows")
        ready = sem("ones_ready")
        negated = sem("edge_weights_negated")
        passed = sem("waits_passed")
        ends_in, edge_in, src_in = each("ends_in"), each("edge_in"), each("src_in")
        s_hot, s_turn, s_hot_t, s_hot_f = each("hot_done"), each("turn_done"), each("hot_t_done"), each("hot_f_done")
        s_prod, s_pre, s_clamp, s_expo = each("prod_done"), each("pre_done"), each("clamp_done"), each("expo_done")
        s_logs, s_gate, s_soft, s_msg = each("logs_done"), each("gate_done"), each("soft_done"), each("msg_done")
        s_sum, s_added = each("sum_done"), each("added")

        max_w = WINDOWS - 1
        win3 = 3 * F2
        block = ctx.enter_context(nc.Block())

        def done(eng, sems, g, j, lag, each_inc=1):
            turns_back = (lag - j + SLOTS - 1) // SLOTS if lag > j else 0
            if isinstance(g, int):
                if g < turns_back:
                    return
                eng.wait_ge(sems[(j - lag) % SLOTS], (g - turns_back + 1) * each_inc)
            elif turns_back == 0:
                eng.wait_ge(sems[j - lag], g * each_inc + each_inc)
            else:
                eng.wait_ge(sems[(j - lag) % SLOTS], (g + (1 - turns_back)) * each_inc)

        def back(g, j, lag):
            turns_back = (lag - j + SLOTS - 1) // SLOTS if lag > j else 0
            if isinstance(g, int) and g < turns_back:
                return None
            return (g + (-turns_back) if turns_back else g), (j - lag) % SLOTS

        def turns(eng, bodies, one, drain):
            for g in range(BODY):
                one(g)
            with eng.Fori(1, bodies) as body:
                for k in range(BODY):
                    one(body * BODY + k if k else body * BODY)
            drain(bodies * BODY)

        def load_windows(eng, engine, first, n):
            return nc.values_load_multi_w_load_instructions(
                wins[:, first:first + n], engines=[engine], min_val=0, max_val=max_w,
                skip_runtime_bounds_check_because="plan_steps clamps every entry to the last window")[1]

        def n_bodies(eng):
            return eng.value_load(t["choice"][:, 0:1], min_val=SORTED_GROUPS // BODY - 1,
                                  max_val=GENERAL_GROUPS // BODY - 1) + 1

        @block.sync
        def _(sp):
            sp.dma_start(w_edge[:], d[f"W{layer}"]["edge"]).then_inc(w_in, 16)
            bodies = n_bodies(sp)
            at = sp.value_load(t["choice"][:, 1:2], min_val=0, max_val=GENERAL_AT - SORTED_AT)
            row = lambda table, first, n: table[bass.ds(first, n)].rearrange("(a c) -> a c", a=1)

            def offsets(n):
                return nc.values_load_multi_w_load_instructions(
                    sp_off[:, 0:n], engines=[mybir.EngineType.SP], min_val=0, max_val=EDGES,
                    skip_runtime_bounds_check_because="plan_steps clamps every entry to the number of edges")[1]

            def load_ends(j, off):
                sp.dma_start(ends[:, j, :, :], d["ends"][bass.ds(off, STEP), :].rearrange(
                    "(p k) c -> p k c", k=TILES)).then_inc(ends_in[j], 16)

            def load_edges(j, off):
                sp.dma_start(edge_t[:, j, :], d["edge_t"][:, bass.ds(off, STEP)]).then_inc(edge_in[j], 16)

            sp.dma_start(sp_off[:, 0:SLOTS], row(t["off_dram"], at + SORTED_AT, SLOTS)).then_inc(sp_tab, 16)
            sp.dma_start(wins[:], row(t["win_dram"], at, BEFORE + SLOTS)).then_inc(win_tab, 16)
            sp.wait_ge(sp_tab, 16)
            offs = offsets(SLOTS)
            sp.dma_start(sp_off[:], row(t["off_dram"], at + SORTED_AT + SLOTS - 1, SLOTS + 1)).then_inc(sp_tab, 16)
            for j in range(SLOTS):
                load_ends(j, offs[j])
                if j < SLOTS - 1:
                    load_edges(j, offs[j])

            def one(g):
                sp.wait_ge(sp_tab, g * 16 + 32)
                sp.sem_inc(passed, 1)
                offs = offsets(SLOTS + 1)
                sp.dma_start(sp_off[:], row(t["off_dram"], at + (g + 1) * SLOTS + (SORTED_AT + SLOTS - 1), SLOTS + 1)
                             ).then_inc(sp_tab, 16)
                for j in range(SLOTS):
                    done(sp, s_hot, g, j, 0)
                    sp.sem_inc(passed, 1)
                    done(sp, src_in, g, j, 0, 32)
                    sp.sem_inc(passed, 1)
                    load_ends(j, offs[j + 1])
                    done(sp, s_prod, g, j, 1)
                    sp.sem_inc(passed, 1)
                    load_edges((j - 1) % SLOTS, offs[j])
                    if j == 0:
                        sp.wait_ge(pe_has, g + 1)
                        sp.wait_ge(dve_has, g + 1)
                        sp.sem_inc(passed, 1)
                        sp.dma_start(wins[:], row(t["win_dram"], at + (g + 1) * SLOTS, BEFORE + SLOTS)
                                     ).then_inc(win_tab, 16)

            for g in range(BODY):
                one(g)
            with sp.Fori(1, bodies - 1) as body:
                for k in range(BODY):
                    one(body * BODY + k if k else body * BODY)
            for k in range(BODY, 1, -1):
                one(bodies * BODY - k)
            groups = bodies * BODY
            sp.wait_ge(sp_tab, groups * 16 + 16)
            sp.sem_inc(passed, 1)
            off, = offsets(1)
            sp.wait_ge(s_prod[SLOTS - 2 + 1], groups + (-1))
            sp.sem_inc(passed, 1)
            load_edges(SLOTS - 1, off)

        @block.gpsimd
        def _(pool):
            nc.gpsimd.memset(msg[:, :, :, F:F + 1], 1.0).then_inc(ready, 1)
            bodies = n_bodies(pool)

            def one(g):
                for pair in range(0, SLOTS, 2):
                    for j in (pair, pair + 1):
                        done(pool, ends_in, g, j, 0, 16)
                    done(pool, s_pre, g, pair + 1, SLOTS)
                    pool.sem_inc(passed, 1)
                    for j in (pair, pair + 1):
                        for k in range(TILES):
                            nc.gpsimd.indirect_dma_start(
                                from_src[:, j, k, :], None, t[f"src_dram{layer}"],
                                bass.IndirectOffsetOnAxis(ap=ends[:, j, k, 0:1], axis=0)).then_inc(src_in[j], 16)
            turns(pool, bodies, one, lambda g: None)

        @block.tensor
        def _(pe):
            bodies = n_bodies(pe)
            pe.wait_ge(negated, 1)

            def turn(g, j):
                done(pe, s_hot, g, j, 0)
                for k in range(TILES):
                    ins = nc.tensor.transpose(turn_ps[:, j % 2, k * P:(k + 1) * P], hot[:, j, k, :], t["ident_b"][:])
                ins.then_inc(s_turn[j], 1)

            def product(g, j, win, last=False):
                done(pe, edge_in, g, j, 0, 16)
                done(pe, s_hot_t, g, j, 0)
                if last:
                    done(pe, s_pre, g, j, 2)
                for k in range(TILES):
                    nc.tensor.matmul(pre_ps[:, j % 2, k, :], edge_t[:, j, k:STEP:TILES], w_edge[:],
                                     start=True, stop=False)
                    for part in range(3):
                        ins = nc.tensor.matmul(pre_ps[:, j % 2, k, :], hot_t[:, j, k, :],
                                               t["dst_parts"][:, bass.ds(win * win3 + part * F2, F2)],
                                               start=False, stop=part == 2)
                ins.then_inc(s_prod[j], 1)

            def window_sum(g, j, last=False):
                done(pe, s_msg, g, j, 0)
                if last:
                    done(pe, s_hot_f, g, j, 0)
                for k in range(TILES):
                    ins = nc.tensor.matmul(sum_ps[:, j % 2, 0:F + 1], hot_f[:, j, k, :], msg[:, j % 2, k, :],
                                           start=k == 0, stop=k == TILES - 1)
                ins.then_inc(s_sum[j], 1)

            def one(g):
                pe.wait_ge(win_tab, g * 16 + 16)
                pe.sem_inc(passed, 1)
                w = load_windows(pe, mybir.EngineType.PE, BEFORE - 1, SLOTS)
                pe.sem_inc(pe_has, 1)
                for j in range(SLOTS):
                    if b := back(g, j, 5):
                        window_sum(*b)
                    turn(g, j)
                    if b := back(g, j, 1):
                        product(*b, w[j])

            def drain(g):
                w = load_windows(pe, mybir.EngineType.PE, BEFORE + SLOTS - 1, 1)
                window_sum(*back(g, 0, 5), last=True)
                product(*back(g, 0, 1), w[0], last=True)
                for step in range(1, 5):
                    window_sum(*back(g + step // SLOTS, step % SLOTS, 5), last=True)
            turns(pe, bodies, one, drain)

        @block.scalar
        def _(act):
            nc.scalar.preload_act_table_set("natural_log_exp_and_others")
            bodies = n_bodies(act)

            def copy_turned(g, j):
                done(act, s_turn, g, j, 0)
                nc.scalar.copy(hot_t[:, j], turn_ps[:, j % 2, 0:TILES * P].rearrange("p (k n) -> p k n", k=TILES)
                               ).then_inc(s_hot_t[j], 1)

            def first_parts(g, j):
                done(act, s_clamp, g, j, 0)
                pairs = pre[:, j].rearrange("p k (h f) -> p k h f", f=F)[:, :, 0:3:2, :]
                nc.scalar.activation(logs[:, j].rearrange("p k (h f) -> p k h f", f=F), pairs, ACT.Exp
                                     ).then_inc(s_expo[j], 1)

            def widen(g, j):
                done(act, s_sum, g, j, SLOTS)
                nc.scalar.copy(hot_f[:, j], hot[:, j]).then_inc(s_hot_f[j], 1)

            def second_part(g, j):
                done(act, s_expo, g, j, 0)
                nc.scalar.activation(logs[:, j], logs[:, j], ACT.Ln, bias=1.0).then_inc(s_logs[j], 1)

            def third_part(g, j):
                done(act, s_logs, g, j, 0)
                nc.scalar.activation(logs[:, j, :, 0:F], logs[:, j, :, 0:F], ACT.Exp, scale=-1.0
                                     ).then_inc(s_gate[j], 1)

            def one(g, live=lambda lag, j: True):
                for j in range(SLOTS):
                    logged = back(g, j, 3) if live(3, j) else None
                    if logged:
                        first_parts(*logged)
                    if live(0, j):
                        copy_turned(g, j)
                    if logged:
                        second_part(*logged)
                    if live(2, j) and (b := back(g, j, 2)):
                        widen(*b)
                    if logged:
                        third_part(*logged)

            def drain(g):
                one(g, lambda lag, j: j < lag)
            turns(act, bodies, one, drain)

        @block.vector
        def _(v):
            nc.vector.memset(t["sums"][:], 0.0).then_inc(ready, 1)
            bodies = n_bodies(v)
            v.wait_ge(w_in, 16)
            nc.vector.tensor_scalar(w_edge[:, 0:F], w_edge[:, 0:F], -1.0, None, ALU.mult).then_inc(negated, 1)
            v.wait_ge(ready, 2)

            def one_hot(g, j, win):
                done(v, ends_in, g, j, 0, 16)
                done(v, s_hot_f, g, j, SLOTS)
                for k in range(TILES):
                    ins = nc.vector.tensor_scalar(hot[:, j, k, :], t["node_no"][:, bass.ds(win * P, P)],
                                                  ends[:, j, k, 1:2], None, ALU.is_equal)
                ins.then_inc(s_hot[j], 1)

            def sums(g, j):
                done(v, s_prod, g, j, 0)
                done(v, src_in, g, j, 0, 32)
                nc.vector.tensor_tensor(pre[:, j, :, 0:F2], pre_ps[:, j % 2], from_src[:, j], ALU.add).then_inc(s_pre[j], 1)

            def clamp(g, j):
                done(v, s_pre, g, j, 0)
                nc.vector.tensor_scalar(pre[:, j, :, F2:3 * F], pre[:, j, :, F:F2], SOFT_MAX, None, ALU.min
                                        ).then_inc(s_clamp[j], 1)

            def softplus(g, j):
                done(v, s_logs, g, j, 0)
                nc.vector.tensor_tensor(logs[:, j, :, F:F2], pre[:, j, :, F:F2], logs[:, j, :, F:F2], ALU.max
                                        ).then_inc(s_soft[j], 1)

            def message(g, j):
                done(v, s_soft, g, j, 0)
                done(v, s_gate, g, j, 0)
                nc.vector.tensor_tensor(msg[:, j % 2, :, 0:F], logs[:, j, :, F:F2], logs[:, j, :, 0:F], ALU.mult
                                        ).then_inc(s_msg[j], 1)

            def add_up(g, j, win, message_runs=True):
                done(v, s_sum, g, j, 0)
                if not message_runs:
                    done(v, s_added, g, j, 1)
                rows = t["sums"][:, bass.ds(win * (F + 1), F + 1)]
                nc.vector.tensor_tensor(rows, sum_ps[:, j % 2, 0:F + 1], rows, ALU.add).then_inc(s_added[j], 1)

            LAST = 6

            def stages(g, j, hot_win, sum_win, live=lambda lag, j: True):
                if live(5, j) and (b := back(g, j, 5)):
                    softplus(*b)
                if live(3, j) and (b := back(g, j, 3)):
                    clamp(*b)
                if live(5, j) and (b := back(g, j, 5)):
                    message(*b)
                if live(LAST, j) and (b := back(g, j, LAST)):
                    add_up(*b, sum_win, live(5, j))
                if live(0, j):
                    one_hot(g, j, hot_win)
                if live(2, j) and (b := back(g, j, 2)):
                    sums(*b)

            def one(g):
                v.wait_ge(win_tab, g * 16 + 16)
                v.sem_inc(passed, 1)
                first = BEFORE - LAST
                w = load_windows(v, mybir.EngineType.DVE, first, BEFORE + SLOTS - first)
                v.sem_inc(dve_has, 1)
                for j in range(SLOTS):
                    stages(g, j, w[LAST + j], w[j])

            def drain(g):
                w = load_windows(v, mybir.EngineType.DVE, BEFORE + SLOTS - LAST, LAST)
                for step in range(LAST):
                    stages(g + step // SLOTS, step % SLOTS, None, w[step], lambda lag, _: step < lag)
                v.wait_ge(s_added[SLOTS - 1], g)
                v.sem_inc(passed, 1)
            turns(v, bodies, one, drain)


def inverse_counts(nc, t, layer):
    with nc.cleanup_on_exit(), ExitStack() as ctx:
        s = nc.alloc_semaphore(f"count_chain{layer}")
        block = ctx.enter_context(nc.Block())

        @block.vector
        def _(v):
            counts = t["sums"][:].rearrange("p (w f) -> p w f", f=F + 1)[:, :, F]
            nc.vector.tensor_scalar(t["per_count"][:, 0:WPAD], counts, 1.0, None, ALU.max).then_inc(s, 1)
            v.wait_ge(s, 1)
            nc.vector.reciprocal(t["per_count"][:, 0:WPAD], t["per_count"][:, 0:WPAD]).then_inc(s, 1)
            v.wait_ge(s, 2)


def finish(nc, t, d, out):
    with nc.cleanup_on_exit(), ExitStack() as ctx:
        sem = lambda name: nc.alloc_semaphore(name)
        sb = lambda name, shape: ctx.enter_context(nc.sbuf_tensor(name, shape, F32))
        CHUNK = 7
        chunks = [range(w, min(w + CHUNK, WINDOWS)) for w in range(0, WINDOWS, CHUNK)]
        neg_mean, var, root = sb("neg_mean", [P, WINDOWS]), sb("var", [P, WINDOWS]), sb("ln_root", [P, WINDOWS])
        eps = sb("ln_eps", [P, 1])
        per_dev, offset = sb("per_dev", [P, WINDOWS]), sb("ln_offset", [P, WINDOWS])
        x_again = [sem(f"x_again{c}") for c in range(len(chunks))]
        shifted, added, scaled, normed, summed, centred = (sem(n) for n in (
            "x_shifted", "x_added", "sums_scaled", "sums_normed", "y_summed", "y_centred"))
        squared, eps_set, rooted, inverted, offset_done, scaled_out, stored = (sem(n) for n in (
            "y_squared", "ln_eps_set", "ln_rooted", "ln_inverted", "ln_offset_done", "y_scaled", "stored"))
        x0 = t["node_no"][:].rearrange("p (w f) -> p w f", f=F)
        y = t["x_nodes"][:].rearrange("p (w f) -> p w f", f=F)
        sums = t["sums"][:].rearrange("p (w f) -> p w f", f=F + 1)[:, :, 0:F]
        block = ctx.enter_context(nc.Block())

        def cols(c):
            return slice(chunks[c][0], chunks[c][-1] + 1)

        def per_feature(vec, c):
            return vec[:].unsqueeze(1).to_broadcast([P, len(chunks[c]), F])

        def per_node(vec, c):
            return vec[:, cols(c)].unsqueeze(2).to_broadcast([P, len(chunks[c]), F])

        @block.sync
        def _(sp):
            for c in range(len(chunks)):
                rows = slice(chunks[c][0] * P, (chunks[c][-1] + 1) * P)
                sp.dma_start(x0[:, cols(c), :], d["x"][rows, :].rearrange("(w p) f -> p w f", p=P)
                             ).then_inc(x_again[c], 16)
            n = 0
            for c in range(len(chunks)):
                sp.wait_ge(scaled_out, c + 1)
                first, last = chunks[c][0], min(chunks[c][-1] + 1, NODES // P)
                if last > first:
                    sp.dma_start(out[first * P:last * P, :].rearrange("(w p) f -> p w f", p=P),
                                 y[:, first:last, :]).then_inc(stored, 16)
                    n += 1
                if last <= chunks[c][-1]:
                    sp.dma_start(out[last * P:NODES, :], y[0:NODES - last * P, last, :]).then_inc(stored, 16)
                    n += 1
            sp.wait_ge(stored, 16 * n)

        @block.gpsimd
        def _(pool):
            for c in range(len(chunks)):
                pool.wait_ge(x_again[c], 16)
                nc.gpsimd.tensor_tensor(x0[:, cols(c), :], x0[:, cols(c), :], per_feature(t["bn_shift2"], c), ALU.add
                                        ).then_inc(shifted, 1)
                pool.wait_ge(shifted, c + 1)
                nc.gpsimd.tensor_tensor(y[:, cols(c), :], y[:, cols(c), :], x0[:, cols(c), :], ALU.add
                                        ).then_inc(added, 1)

        @block.vector
        def _(v):
            tt = nc.vector.tensor_tensor
            nc.vector.memset(eps[:], LN_EPS).then_inc(eps_set, 1)
            for c in range(len(chunks) + 1):
                here, before = c < len(chunks), c > 0
                if here:
                    tt(sums[:, cols(c), :], sums[:, cols(c), :], per_node(t["per_count"], c), ALU.mult
                       ).then_inc(scaled, 1)
                    v.wait_ge(scaled, c + 1)
                    tt(sums[:, cols(c), :], sums[:, cols(c), :], per_feature(t["bn_scale2"], c), ALU.mult
                       ).then_inc(normed, 1)
                if here:
                    v.wait_ge(normed, c + 1)
                    v.wait_ge(added, c + 1)
                    tt(y[:, cols(c), :], y[:, cols(c), :], sums[:, cols(c), :], ALU.add).then_inc(summed, 1)
                if before:
                    v.wait_ge(rooted, c)
                    nc.vector.reciprocal(per_dev[:, cols(c - 1)], root[:, cols(c - 1)]).then_inc(inverted, 1)
                if here:
                    v.wait_ge(summed, 2 * c + 1)
                    nc.vector.tensor_reduce(neg_mean[:, cols(c)], y[:, cols(c), :], AX.X, ALU.add).then_inc(summed, 1)
                if before:
                    v.wait_ge(inverted, c)
                    tt(offset[:, cols(c - 1)], neg_mean[:, cols(c - 1)], per_dev[:, cols(c - 1)], ALU.mult
                       ).then_inc(offset_done, 1)
                if here:
                    v.wait_ge(summed, 2 * c + 2)
                    nc.vector.tensor_scalar(neg_mean[:, cols(c)], neg_mean[:, cols(c)], -1.0 / F, None, ALU.mult
                                            ).then_inc(centred, 1)

        @block.scalar
        def _(act):
            act.wait_ge(eps_set, 1)
            for c in range(len(chunks) + 1):
                if c < len(chunks):
                    act.wait_ge(centred, c + 1)
                    for w in chunks[c]:
                        ins = nc.scalar.activation(sums[:, w, :], y[:, w, :], ACT.Square, bias=neg_mean[:, w:w + 1],
                                                   accum_out=var[:, w:w + 1])
                    ins.then_inc(squared, 1)
                    act.wait_ge(squared, c + 1)
                    nc.scalar.activation(root[:, cols(c)], var[:, cols(c)], ACT.Sqrt, bias=eps[:], scale=1.0 / F
                                         ).then_inc(rooted, 1)
                if c > 0:
                    act.wait_ge(offset_done, c)
                    for w in chunks[c - 1]:
                        ins = nc.scalar.activation(y[:, w, :], y[:, w, :], ACT.Identity, bias=offset[:, w:w + 1],
                                                   scale=per_dev[:, w:w + 1])
                    ins.then_inc(scaled_out, 1)


def graph_layers(nc, d, out):
    with ExitStack() as ctx:
        sb = lambda name, shape, dt: ctx.enter_context(nc.sbuf_tensor(name, shape, dt))
        ctx.enter_context(nc.allow_non_contiguous_dma(reason="16-byte rows of edge ends, and small tables"))
        t = {
            "off_dram": nc.dram_tensor("off_table", [TABLE], I32, kind="Internal").ap(),
            "win_dram": nc.dram_tensor("win_table", [TABLE], I32, kind="Internal").ap(),
            "src_dram1": nc.dram_tensor("src_rows1", [NPAD, F2], F32, kind="Internal").ap(),
            "src_dram2": nc.dram_tensor("src_rows2", [NPAD, F2], F32, kind="Internal").ap(),
            "choice": sb("choice", [1, 2], I32),
            "node_no": sb("node_no", [P, WINDOWS * P], F32),
            "sums": sb("sums", [P, WPAD * (F + 1)], F32),
            "per_count": sb("per_count", [P, WPAD], F32),
            "ident": sb("ident", [P, P], F32),
            "ident_b": sb("ident_b", [P, P], BF16),
            "bn_scale1": sb("bn_scale1", [P, F], F32), "bn_shift1": sb("bn_shift1", [P, F], F32),
            "bn_scale2": sb("bn_scale2", [P, F], F32), "bn_shift2": sb("bn_shift2", [P, F], F32),
        }
        t["x_nodes"] = sb("x_nodes", [P, WPAD * F], F32)
        plan_steps(nc, t, d)
        t["dst_parts"] = sb("dst_parts", [P, WPAD * 3 * F2], BF16)
        layer_tables(nc, t, d, 1)
        edge_loop(nc, t, d, 1)
        inverse_counts(nc, t, 1)
        layer_tables(nc, t, d, 2)
        edge_loop(nc, t, d, 2)
        finish(nc, t, d, out)


def kernel(**inputs):
    import concourse.bacc as bacc
    from concourse.bass_utils import run_bass_kernel_spmd

    a = {k: np.asarray(v) for k, v in inputs.items()}
    nc = bacc.Bacc("TRN2", target_bir_lowering=False, num_devices=1)
    arrays = {}

    def given(name, array):
        array = np.ascontiguousarray(array)
        arrays[name] = array
        return nc.dram_tensor(name, array.shape, mybir.dt.from_np(array.dtype), kind="ExternalInput").ap()

    x = np.zeros((NPAD, F), a["x"].dtype)
    x[:NODES] = a["x"]
    ends = np.zeros((EPAD, 2), a["src"].dtype)
    ends[:, 1] = NO_WINDOW
    ends[:EDGES, 0] = a["src"]
    ends[:EDGES, 1] = a["dst"]
    dst = np.full((EPAD + P,), NO_WINDOW, a["dst"].dtype)
    dst[:EDGES] = a["dst"]
    edge_t = np.zeros((FE, EPAD), a["edge_attr_64"].dtype)
    edge_t[:, :EDGES] = a["edge_attr_64"].T
    d = {
        "x": given("x_rows", x), "xT": given("x_cols", x.T), "ends": given("edge_ends", ends),
        "dst": given("destinations", dst), "edge_t": given("edge_cols", edge_t),
    }
    for layer in (1, 2):
        p = {k: a[f"L0_gnn_{k}{layer}"] for k in ("Wf", "bf", "Ws", "bs", "gamma", "beta", "rmean", "rvar")}
        both = np.concatenate([p["Wf"], p["Ws"]], axis=1)
        d[f"W{layer}"] = {
            "node": given(f"in_w_node{layer}", np.concatenate([both[:F], both[F:2 * F]], axis=1)),
            "edge": given(f"in_w_edge{layer}", both[2 * F:]),
            "bias": given(f"in_bias{layer}", np.concatenate([p["bf"], p["bs"]])),
            **{k: given(f"{k}{layer}", p[k]) for k in ("gamma", "beta", "rmean", "rvar")},
        }
    out = nc.dram_tensor("out", (NODES, F), F32, kind="ExternalOutput").ap()
    graph_layers(nc, d, out)
    r = run_bass_kernel_spmd(nc, [arrays], core_ids=[0])
    return r.results[0]["out"]
```
